# Optimizing a Trainium2 kernel written in Bass

```python
import numpy as np
import jax
import jax.numpy as jnp

def _softmax(x, axis=-1):
    return jax.nn.softmax(x, axis=axis)

def _gelu(x):
    return jax.nn.gelu(x, approximate=True)

def _silu(x):
    return jax.nn.silu(x)

def _sigmoid(x):
    return jax.nn.sigmoid(x)

def _layernorm(x, axis=-1, eps=1e-05):
    m = jnp.mean(x, axis=axis, keepdims=True)
    v = jnp.var(x, axis=axis, keepdims=True)
    return (x - m) / jnp.sqrt(v + eps)

def _scatter_add(tgt, idx, src, axis=0):
    return tgt.at[idx].add(src)

def _segment_sum(src, seg, n):
    return jax.ops.segment_sum(src, seg, n)
kernel_name = 'mk_gnn_preln_d2_gnn_r8_3482e6'

def setup_inputs(seed: int=0):
    np.random.seed(seed)
    _w = jnp.asarray

    def _rec_inputs():
        import jax
        import jax.numpy as jnp
        _gk = jax.random.key(seed)
        x = -0.0002117 + 1 * jax.random.normal(jax.random.fold_in(_gk, 1), (6250, 512), jnp.float32)
        src = jax.random.randint(jax.random.fold_in(_gk, 2), (100000,), 0, 6250, jnp.int32)
        dst = jnp.minimum((6250 * jax.random.uniform(jax.random.fold_in(_gk, 3), (100000,)) ** 2.0).astype(jnp.int32), 49999)
        _o = jnp.argsort(dst, stable=True)
        src = src[_o]
        dst = dst[_o]
        edge_attr_4 = 0.00171547 + 0.999346 * jax.random.normal(jax.random.fold_in(_gk, 11), (100000, 4), jnp.float32)
        edge_attr_8 = 0.000126197 + 0.999763 * jax.random.normal(jax.random.fold_in(_gk, 12), (100000, 8), jnp.float32)
        return (x, src, dst, edge_attr_4, edge_attr_8)
    x, src, dst, edge_attr_4, edge_attr_8 = _rec_inputs()

    def _L0_gnn_setup():
        import jax, jax.numpy as jnp
        import numpy as np
        from math import sqrt
        N_NODES = 6250
        N_EDGES = 50000
        D_EMB = 512
        HEADS = 8
        DK = 32
        DV = 32
        key = jax.random.key(seed)
        ks = jax.random.split(key, 8)
        x = jax.random.normal(ks[0], (N_NODES, D_EMB), dtype=jnp.float32)
        edge_index = jax.random.randint(ks[1], (2, N_EDGES), 0, N_NODES, dtype=jnp.int64)

        def lin(k, fan_in, fan_out):
            bound = 1.0 / sqrt(fan_in)
            kw, kb = jax.random.split(k)
            W = jax.random.uniform(kw, (fan_in, fan_out), minval=-bound, maxval=bound, dtype=jnp.float32)
            b = jax.random.uniform(kb, (fan_out,), minval=-bound, maxval=bound, dtype=jnp.float32)
            return (W, b)
        Wk, bk = lin(ks[2], D_EMB, HEADS * DK)
        Wq, bq = lin(ks[3], D_EMB, HEADS * DK)
        Wv, bv = lin(ks[4], D_EMB, HEADS * DV)
        Wa, ba = lin(ks[5], HEADS * DV, D_EMB)
        Wf, bf = lin(ks[6], D_EMB, D_EMB)
        return {'x': x, 'edge_index': edge_index, 'Wk': Wk, 'bk': bk, 'Wq': Wq, 'bq': bq, 'Wv': Wv, 'bv': bv, 'Wa': Wa, 'ba': ba, 'Wf': Wf, 'bf': bf}
    _L0_gnn_all = _L0_gnn_setup()
    _L0_gnn_in = {k: v for k, v in _L0_gnn_all.items() if k in ('Wk', 'bk', 'Wq', 'bq', 'Wv', 'bv', 'Wa', 'ba', 'Wf', 'bf')}
    del _L0_gnn_all

    def _L1_gnn_setup():
        import jax, jax.numpy as jnp
        import numpy as np
        MUL = 128
        N_NODES = 1250
        N_EDGES = 20000
        R_BASIS = 8
        HIDDEN = 64
        W_NUMEL = 4 * MUL
        SQRT3 = 3.0 ** 0.5
        SILU_2MOM = 1.679177
        AVG_NUM_NEIGHBORS = 10.0

        def _lin_irreps(x0, x1, W0, W1):
            y0 = x0 @ W0 / jnp.sqrt(jnp.float32(W0.shape[0]))
            y1 = jnp.einsum('num,uv->nvm', x1, W1) / jnp.sqrt(jnp.float32(W1.shape[0]))
            return (y0, y1)

        def _forward(node_feats, edge_attrs, edge_feats, edge_index, W_up0, W_up1, W_mlp1, W_mlp2, W_mlp3, W_mlp4, W_out0, W_out1):
            num_nodes = node_feats.shape[0]
            sender, receiver = (edge_index[0], edge_index[1])
            x0 = node_feats[:, :MUL]
            x1 = node_feats[:, MUL:].reshape(num_nodes, MUL, 3)
            x0, x1 = _lin_irreps(x0, x1, W_up0, W_up1)
            h = edge_feats
            for W in (W_mlp1, W_mlp2, W_mlp3):
                h = SILU_2MOM * jax.nn.silu(h @ W / jnp.sqrt(jnp.float32(W.shape[0])))
            tpw = h @ W_mlp4 / jnp.sqrt(jnp.float32(W_mlp4.shape[0]))
            w1, w2, w3, w4 = jnp.split(tpw, 4, axis=-1)
            s0 = x0[sender]
            s1 = x1[sender]
            y0 = edge_attrs[:, 0:1]
            y1 = edge_attrs[:, 1:4]
            p1 = w1 * s0 * y0
            p2 = (w2 * s0)[:, :, None] * y1[:, None, :]
            p3 = w3[:, :, None] * s1 * y0[:, None, :]
            p4 = w4 * jnp.einsum('eum,em->eu', s1, y1) / SQRT3
            m0 = jnp.concatenate([p1, p4], axis=-1)
            m1 = jnp.concatenate([p2, p3], axis=1)
            msg0 = jax.ops.segment_sum(m0, receiver, num_segments=num_nodes)
            msg1 = jax.ops.segment_sum(m1, receiver, num_segments=num_nodes)
            o0, o1 = _lin_irreps(msg0, msg1, W_out0, W_out1)
            out = jnp.concatenate([o0, o1.reshape(num_nodes, 3 * MUL)], axis=-1)
            return out / AVG_NUM_NEIGHBORS
        key = jax.random.key(seed)
        ks = jax.random.split(key, 12)
        rn = lambda k, s: jax.random.normal(k, s, dtype=jnp.float32)
        return {'node_feats': rn(ks[0], (N_NODES, 4 * MUL)), 'edge_attrs': rn(ks[1], (N_EDGES, 4)), 'edge_feats': rn(ks[2], (N_EDGES, R_BASIS)), 'edge_index': jax.random.randint(ks[3], (2, N_EDGES), 0, N_NODES), 'W_up0': rn(ks[4], (MUL, MUL)), 'W_up1': rn(ks[5], (MUL, MUL)), 'W_mlp1': rn(ks[6], (R_BASIS, HIDDEN)), 'W_mlp2': rn(ks[7], (HIDDEN, HIDDEN)), 'W_mlp3': rn(ks[8], (HIDDEN, HIDDEN)), 'W_mlp4': rn(ks[9], (HIDDEN, W_NUMEL)), 'W_out0': rn(ks[10], (2 * MUL, MUL)), 'W_out1': rn(ks[11], (2 * MUL, MUL))}
    _L1_gnn_all = _L1_gnn_setup()
    _L1_gnn_in = {k: v for k, v in _L1_gnn_all.items() if k in ('W_up0', 'W_up1', 'W_mlp1', 'W_mlp2', 'W_mlp3', 'W_mlp4', 'W_out0', 'W_out1')}
    del _L1_gnn_all
    return {'x': x, 'src': src, 'dst': dst, 'edge_attr_4': edge_attr_4, 'edge_attr_8': edge_attr_8, 'L0_gnn_Wk': _L0_gnn_in['Wk'], 'L0_gnn_bk': _L0_gnn_in['bk'], 'L0_gnn_Wq': _L0_gnn_in['Wq'], 'L0_gnn_bq': _L0_gnn_in['bq'], 'L0_gnn_Wv': _L0_gnn_in['Wv'], 'L0_gnn_bv': _L0_gnn_in['bv'], 'L0_gnn_Wa': _L0_gnn_in['Wa'], 'L0_gnn_ba': _L0_gnn_in['ba'], 'L0_gnn_Wf': _L0_gnn_in['Wf'], 'L0_gnn_bf': _L0_gnn_in['bf'], 'L1_gnn_W_up0': _L1_gnn_in['W_up0'], 'L1_gnn_W_up1': _L1_gnn_in['W_up1'], 'L1_gnn_W_mlp1': _L1_gnn_in['W_mlp1'], 'L1_gnn_W_mlp2': _L1_gnn_in['W_mlp2'], 'L1_gnn_W_mlp3': _L1_gnn_in['W_mlp3'], 'L1_gnn_W_mlp4': _L1_gnn_in['W_mlp4'], 'L1_gnn_W_out0': _L1_gnn_in['W_out0'], 'L1_gnn_W_out1': _L1_gnn_in['W_out1']}

def reference(x, src, dst, edge_attr_4, edge_attr_8, L0_gnn_Wk, L0_gnn_bk, L0_gnn_Wq, L0_gnn_bq, L0_gnn_Wv, L0_gnn_bv, L0_gnn_Wa, L0_gnn_ba, L0_gnn_Wf, L0_gnn_bf, L1_gnn_W_up0, L1_gnn_W_up1, L1_gnn_W_mlp1, L1_gnn_W_mlp2, L1_gnn_W_mlp3, L1_gnn_W_mlp4, L1_gnn_W_out0, L1_gnn_W_out1):
    import jax
    import jax.numpy as jnp

    def _L0_gnn_ref(x, edge_index, Wk, bk, Wq, bq, Wv, bv, Wa, ba, Wf, bf):
        import jax, jax.numpy as jnp
        import numpy as np
        from math import sqrt
        N_NODES = 6250
        N_EDGES = 50000
        D_EMB = 512
        HEADS = 8
        DK = 32
        DV = 32
        N = x.shape[0]
        receivers, senders = (edge_index[0], edge_index[1])
        K = (x @ Wk + bk).reshape(N, HEADS, DK)
        Q = (x @ Wq + bq).reshape(N, HEADS, DK)
        V = (x @ Wv + bv).reshape(N, HEADS, DV)
        att = jnp.exp(jnp.einsum('ehd,ehd->eh', Q[receivers], K[senders]) / sqrt(DK))
        denom = jax.ops.segment_sum(att, receivers, num_segments=N)
        att = att / denom[receivers]
        msg = att[:, :, None] * V[senders]
        agg = jnp.zeros((N, HEADS, DV), dtype=V.dtype).at[receivers].add(msg)
        out = jax.nn.relu(agg).reshape(N, HEADS * DV)
        out = jax.nn.relu(out @ Wa + ba)
        out = jax.nn.relu(out @ Wf + bf)
        return x + out

    def _L1_gnn_ref(node_feats, edge_attrs, edge_feats, edge_index, W_up0, W_up1, W_mlp1, W_mlp2, W_mlp3, W_mlp4, W_out0, W_out1):
        import jax, jax.numpy as jnp
        import numpy as np
        MUL = 128
        N_NODES = 1250
        N_EDGES = 20000
        R_BASIS = 8
        HIDDEN = 64
        W_NUMEL = 4 * MUL
        SQRT3 = 3.0 ** 0.5
        SILU_2MOM = 1.679177
        AVG_NUM_NEIGHBORS = 10.0

        def _lin_irreps(x0, x1, W0, W1):
            y0 = x0 @ W0 / jnp.sqrt(jnp.float32(W0.shape[0]))
            y1 = jnp.einsum('num,uv->nvm', x1, W1) / jnp.sqrt(jnp.float32(W1.shape[0]))
            return (y0, y1)

        def _forward(node_feats, edge_attrs, edge_feats, edge_index, W_up0, W_up1, W_mlp1, W_mlp2, W_mlp3, W_mlp4, W_out0, W_out1):
            num_nodes = node_feats.shape[0]
            sender, receiver = (edge_index[0], edge_index[1])
            x0 = node_feats[:, :MUL]
            x1 = node_feats[:, MUL:].reshape(num_nodes, MUL, 3)
            x0, x1 = _lin_irreps(x0, x1, W_up0, W_up1)
            h = edge_feats
            for W in (W_mlp1, W_mlp2, W_mlp3):
                h = SILU_2MOM * jax.nn.silu(h @ W / jnp.sqrt(jnp.float32(W.shape[0])))
            tpw = h @ W_mlp4 / jnp.sqrt(jnp.float32(W_mlp4.shape[0]))
            w1, w2, w3, w4 = jnp.split(tpw, 4, axis=-1)
            s0 = x0[sender]
            s1 = x1[sender]
            y0 = edge_attrs[:, 0:1]
            y1 = edge_attrs[:, 1:4]
            p1 = w1 * s0 * y0
            p2 = (w2 * s0)[:, :, None] * y1[:, None, :]
            p3 = w3[:, :, None] * s1 * y0[:, None, :]
            p4 = w4 * jnp.einsum('eum,em->eu', s1, y1) / SQRT3
            m0 = jnp.concatenate([p1, p4], axis=-1)
            m1 = jnp.concatenate([p2, p3], axis=1)
            msg0 = jax.ops.segment_sum(m0, receiver, num_segments=num_nodes)
            msg1 = jax.ops.segment_sum(m1, receiver, num_segments=num_nodes)
            o0, o1 = _lin_irreps(msg0, msg1, W_out0, W_out1)
            out = jnp.concatenate([o0, o1.reshape(num_nodes, 3 * MUL)], axis=-1)
            return out / AVG_NUM_NEIGHBORS
        return _forward(node_feats, edge_attrs, edge_feats, edge_index, W_up0, W_up1, W_mlp1, W_mlp2, W_mlp3, W_mlp4, W_out0, W_out1)
    edge_index = jnp.stack([src, dst])
    h = jnp.maximum(_layernorm(x, axis=-1), 0.0)
    x = x + _L0_gnn_ref(h, edge_index, L0_gnn_Wk, L0_gnn_bk, L0_gnn_Wq, L0_gnn_bq, L0_gnn_Wv, L0_gnn_bv, L0_gnn_Wa, L0_gnn_ba, L0_gnn_Wf, L0_gnn_bf)
    h = jnp.maximum(_layernorm(x, axis=-1), 0.0)
    x = x + _L1_gnn_ref(h, edge_attr_4, edge_attr_8, edge_index, L1_gnn_W_up0, L1_gnn_W_up1, L1_gnn_W_mlp1, L1_gnn_W_mlp2, L1_gnn_W_mlp3, L1_gnn_W_mlp4, L1_gnn_W_out0, L1_gnn_W_out1)
    return x

_drawn_inputs = setup_inputs


def setup_inputs(seed=0):
    import zlib

    import numpy as np

    out = dict(_drawn_inputs(seed))
    spreads = {}
    factors = {'L0_gnn_Wk': 8.0,
     'L0_gnn_bk': 8.0,
     'L0_gnn_Wq': 8.0,
     'L0_gnn_bq': 8.0,
     'L0_gnn_Wv': 5.082,
     'L0_gnn_bv': 8.0,
     'L0_gnn_Wa': 4.644,
     'L0_gnn_ba': 8.0,
     'L0_gnn_Wf': 3.519,
     'L0_gnn_bf': 5.472}
    for name, (base, spread) in spreads.items():
        noise = np.random.default_rng([zlib.crc32(name.encode()), seed]).standard_normal(out[name].shape)
        drawn = base * np.exp(spread * noise) if base else spread * noise
        out[name] = jnp.asarray(drawn.astype(out[name].dtype))
    for name, factor in factors.items():
        out[name] = (out[name] * factor).astype(out[name].dtype)
    return out
```

```python
from contextlib import ExitStack

import concourse.bass as bass
from concourse import mybir

ALU = mybir.AluOpType
ACT = mybir.ActivationFunctionType
AX = mybir.AxisListType
F32 = mybir.dt.float32
F32R = mybir.dt.float32r
I32 = mybir.dt.int32

P = 128
D = 512
H, DK = 8, 32
HD = H * DK
AW = HD + H
MUL = 128
HID = 64
RB = 8
MW = 8 * MUL
U = 4
NREP = 2
EPS = 1e-5
SILU_2MOM = 1.679177


def node_rows(n):
    full = -(-n // P) * P + P
    return -(-full // (2 * P)) * 2 * P


def edge_rows(n):
    return -(-n // (2 * U * P)) * 2 * U * P


def after(eng, sem, value):
    if not isinstance(value, int) or value > 0:
        eng.wait_ge(sem, value)


def held(eng, passed):
    eng.sem_inc(passed, 1)


def software_pipeline(eng, tiles, unroll, stages):
    rounds = tiles // unroll
    start = 1 + -(-max(lag for lag, _ in stages) // unroll)
    for t in range(start * unroll):
        for lag, stage in stages:
            if t >= lag:
                stage((t - lag) // unroll, (t - lag) % unroll)
    with eng.Fori(start, rounds) as i:
        for j in range(unroll):
            for lag, stage in stages:
                back = (j - lag) // unroll
                stage(i + back if back else i, (j - lag) % unroll)
    for t in range(tiles, tiles + max(lag for lag, _ in stages)):
        for lag, stage in stages:
            if t - lag < tiles:
                stage((t - lag) // unroll, (t - lag) % unroll)


def by_path(eng, wide, program):
    flag = eng.value_load(wide[0:1, 0:1], min_val=0, max_val=1)
    with eng.If(flag > 0):
        program(eng, False)
    with eng.Else():
        program(eng, True)


class Space:

    def __init__(self, nc, ctx, prefix):
        self.nc, self.ctx, self.prefix = nc, ctx, prefix

    def sb(self, name, shape, dt=F32):
        return self.ctx.enter_context(self.nc.sbuf_tensor(self.prefix + name, shape, dt))

    def ps(self, name, shape):
        return self.ctx.enter_context(self.nc.psum_tensor(self.prefix + name, shape, F32))

    def sem(self, name):
        return self.ctx.enter_context(self.nc.semaphore(self.prefix + name))


def build_setup(nc, w, dram, n_rows, groups):
    half_groups = groups // 2
    with ExitStack() as ctx:
        s = Space(nc, ctx, "su_")
        mlp4 = s.sb("mlp4", [P, 4 * MUL])
        wout = s.sb("wout", [P, 4, MUL])
        send = s.sb("send", [half_groups, 2, U * P], I32)
        least = s.sb("least", [half_groups, 2])
        most = s.sb("most", [half_groups, 2])
        least_i = s.sb("least_i", [half_groups, 2], I32)
        span_i = s.sb("span_i", [half_groups, 2], I32)
        spans = s.sb("spans", [1, groups], I32)
        widest = s.sb("widest", [1, 1])
        iota_i = s.sb("iota_i", [P, P], I32)
        part_i = s.sb("part_i", [P, 1], I32)
        part_f = s.sb("part_f", [P, 1])
        spare_i = s.sb("spare_i", [P, 1], I32)
        loaded, cleared, made, send_in, least_ready, most_ready, base_ready, span_ready, base_out, base_in, \
            widest_ready, window_ready, split = (s.sem(n) for n in (
                "loaded", "cleared", "made", "send_in", "least_ready", "most_ready", "base_ready", "span_ready",
                "base_out", "base_in", "widest_ready", "window_ready", "split"))
        block = ctx.enter_context(nc.Block())
        N_LOADED = 3 + 3 + 4 + 2 + 2 + 2 + 4 + 4

        @block.sync
        def _(sync):
            sync.dma_start(send[:, :, :], dram["dst_row"].rearrange("(p c) a e -> p (c a) e", c=2)).then_inc(send_in, 16)
            for t, name in enumerate(("L0_gnn_Wq", "L0_gnn_Wk", "L0_gnn_Wv")):
                sync.dma_start(w["wqkv"][:, :, t * HD:(t + 1) * HD],
                               dram[name].rearrange("(c p) n -> p c n", p=P)).then_inc(loaded, 16)
            for t, name in enumerate(("L0_gnn_bq", "L0_gnn_bk", "L0_gnn_bv")):
                sync.dma_start(w["bqkv"][:, t * HD:(t + 1) * HD],
                               dram[name].rearrange("(a n) -> a n", a=1).to_broadcast([P, HD])).then_inc(loaded, 16)
            sync.dma_start(w["bf"][:, :],
                           dram["L0_gnn_bf"].rearrange("(a n) -> a n", a=1).to_broadcast([P, D])).then_inc(loaded, 16)
            sync.dma_start(w["ba"][:, :], dram["L0_gnn_ba"].rearrange("(c p) -> p c", p=P),
                           allow_slow_non_contiguous=True).then_inc(loaded, 16)
            sync.dma_start(w["wa"][:, :, :], dram["L0_gnn_Wa"].rearrange("(c p) n -> p c n", p=P)).then_inc(loaded, 16)
            sync.dma_start(w["wf"][:, :, :], dram["L0_gnn_Wf"].rearrange("(c p) n -> p c n", p=P)).then_inc(loaded, 16)
            sync.wait_ge(base_ready, 1)
            sync.dma_start(dram["base"].rearrange("a (p c) -> (a p) c", c=2), least_i[:, :]).then_inc(base_out, 16)
            sync.wait_ge(span_ready, 1)
            sync.dma_start(dram["span"].rearrange("a (p c) -> (a p) c", c=2), span_i[:, :]).then_inc(base_out, 16)
            sync.wait_ge(base_out, 32)
            sync.dma_start(w["base"][:, :], dram["base"].to_broadcast([P, groups])).then_inc(base_in, 16)
            sync.dma_start(spans[:, :], dram["span"]).then_inc(base_in, 16)

        @block.scalar
        def _(act):
            act.dma_start(w["wup"][:, 0, :], dram["L1_gnn_W_up0"]).then_inc(loaded, 16)
            act.dma_start(w["wup"][:, 1, :], dram["L1_gnn_W_up1"]).then_inc(loaded, 16)
            act.dma_start(wout[:, 0:2, :], dram["L1_gnn_W_out0"].rearrange("(c p) n -> p c n", p=P)).then_inc(loaded, 16)
            act.dma_start(wout[:, 2:4, :], dram["L1_gnn_W_out1"].rearrange("(c p) n -> p c n", p=P)).then_inc(loaded, 16)
            act.wait_ge(cleared, 3)
            for half in range(2):
                lo, hi = half * HID, (half + 1) * HID
                act.dma_start(mlp4[lo:hi, :], dram["L1_gnn_W_mlp4"]).then_inc(loaded, 16)
                act.dma_start(w["mlp1"][half * RB:(half + 1) * RB, lo:hi], dram["L1_gnn_W_mlp1"]).then_inc(loaded, 16)
                act.dma_start(w["mlp2"][lo:hi, lo:hi], dram["L1_gnn_W_mlp2"]).then_inc(loaded, 16)
                for copy in range(2):
                    act.dma_start(w["mlp3"][lo:hi, half, copy * HID:(copy + 1) * HID], dram["L1_gnn_W_mlp3"]).then_inc(loaded, 16)
            act.wait_ge(loaded, 16 * N_LOADED)

        @block.gpsimd
        def _(pool):
            pool.memset(w["mlp1"][:, :], 0.0).then_inc(cleared, 1)
            pool.memset(w["mlp2"][:, :], 0.0).then_inc(cleared, 1)
            pool.memset(w["mlp3"][:, :, :], 0.0).then_inc(cleared, 1)
            pool.memset(w["ident"][:, :], 0.0).then_inc(made, 1)
            pool.memset(w["before"][:, :], 1.0).then_inc(made, 1)
            pool.memset(w["zeros"][:, :], 0.0).then_inc(made, 1)
            pool.wait_ge(made, 3)
            pool.affine_select(out=w["ident"][:, :], in_=w["ident"][:, :], compare_op=ALU.not_equal, fill=1.0,
                               base=0, pattern=[[-1, P]], channel_multiplier=1).then_inc(made, 1)
            pool.affine_select(out=w["before"][:, :], in_=w["before"][:, :], compare_op=ALU.is_gt, fill=0.0,
                               base=0, pattern=[[-1, P]], channel_multiplier=1).then_inc(made, 1)
            pool.iota(spare_i[:, :], pattern=[[0, 1]], base=n_rows - P, channel_multiplier=1).then_inc(made, 1)
            pool.iota(iota_i[:, :], pattern=[[1, P]], base=0, channel_multiplier=0).then_inc(made, 1)
            pool.iota(part_i[:, :], pattern=[[0, 1]], base=0, channel_multiplier=1).then_inc(made, 1)

        @block.vector
        def _(dve):
            dve.memset(w["eps"][:, :], EPS)
            dve.wait_ge(send_in, 16)
            dve.tensor_reduce(least[:, :], send[:, :, :], AX.X, ALU.min).then_inc(least_ready, 1)
            dve.tensor_reduce(most[:, :], send[:, :, :], AX.X, ALU.max).then_inc(most_ready, 1)
            dve.wait_ge(least_ready, 1)
            dve.tensor_copy(least_i[:, :], least[:, :]).then_inc(base_ready, 1)
            dve.wait_ge(most_ready, 1)
            dve.tensor_tensor(span_i[:, :], most[:, :], least[:, :], ALU.subtract).then_inc(span_ready, 1)
            dve.wait_ge(made, 8)
            dve.tensor_copy(w["spare_f"][:, :], spare_i[:, :])
            dve.tensor_copy(w["iota_f"][:, :], iota_i[:, :])
            dve.tensor_copy(part_f[:, :], part_i[:, :]).then_inc(window_ready, 1)
            dve.wait_ge(base_in, 32)
            dve.tensor_copy(w["first_of"][:, :], w["base"][:, :]).then_inc(window_ready, 1)
            dve.tensor_reduce(widest[:, :], spans[:, :], AX.X, ALU.max).then_inc(widest_ready, 1)
            dve.wait_ge(window_ready, 2)
            dve.tensor_scalar(w["node_of"][:, :], w["first_of"][:, :], part_f[:, 0:1], None, ALU.add).then_inc(window_ready, 1)
            dve.wait_ge(widest_ready, 1)
            dve.tensor_scalar(w["wide"][:, :], widest[:, :], float(P), None, ALU.is_ge)
            dve.wait_ge(loaded, 16 * N_LOADED)
            dve.tensor_copy(w["mlp4_hi"][:, :], mlp4[:, :]).then_inc(split, 1)
            dve.wait_ge(split, 1)
            dve.tensor_tensor(w["mlp4_lo"][:, :], mlp4[:, :], w["mlp4_hi"][:, :].bitcast(F32), ALU.subtract)
            k = (SILU_2MOM / HID ** 0.5) / (2 * MUL) ** 0.5 / 10.0
            for c, factor in enumerate((k, k / 3.0 ** 0.5, k, k)):
                dve.tensor_scalar(w["wout"][:, c, :], wout[:, c, :], factor, None, ALU.mult)


def build_project(nc, w, dram, n_rows):
    tiles = n_rows // P
    with ExitStack() as ctx:
        s = Space(nc, ctx, "pj_")
        x = s.sb("x", [P, 2, D])
        h = s.sb("h", [P, 2, D])
        hT = s.sb("hT", [P, 2, D])
        q_out = s.sb("q_out", [P, 2, HD])
        kv_out = s.sb("kv_out", [P, 2, 2 * HD])
        stats = s.sb("stats", [P, 2, 6])
        mv = s.sb("mv", [P, 2, 2])
        std = s.sb("std", [P, 2, 1])
        rstd = s.sb("rstd", [P, 2, 1])
        shift = s.sb("shift", [P, 2, 1])
        ps_t = [s.ps(f"ps_t{j}", [P, D]) for j in range(2)]
        ps_q = [s.ps(f"ps_q{j}", [P, HD]) for j in range(2)]
        ps_kv = [s.ps(f"ps_kv{j}", [P, 2 * HD]) for j in range(2)]
        x_in = [s.sem(f"x_in{j}") for j in range(2)]
        out_q = [s.sem(f"out_q{j}") for j in range(2)]
        out_kv = [s.sem(f"out_kv{j}") for j in range(2)]
        zeroed = s.sem("zeroed")
        (stats_ready, mv_ready, std_ready, rstd_ready, shift_ready, h_ready, xh_ready, turned, hT_ready,
         multiplied, q_ready, kv_ready) = (s.sem(n) for n in (
             "stats_ready", "mv_ready", "std_ready", "rstd_ready", "shift_ready", "h_ready", "xh_ready", "turned",
             "hT_ready", "multiplied", "q_ready", "kv_ready"))
        dve_passed = s.sem("dve_passed")
        block = ctx.enter_context(nc.Block())

        @block.sync
        def _(sync):
            def load(i, j):
                t = 2 * i + j
                after(sync, h_ready, t - 1)
                after(sync, xh_ready, t - 1)
                sync.dma_start(x[:, j, :], dram["x"][t, :, :]).then_inc(x_in[j], 16)

            def clear(i, j):
                t = 2 * i + j
                for table in dram["att_sum_t"]:
                    sync.dma_start(table[t, :, :], w["zeros"][:, 0:AW]).then_inc(zeroed, 16)
                sync.dma_start(dram["msg_sum_t"][t, :, :], w["zeros"][:, :]).then_inc(zeroed, 16)

            def store(i, j):
                t = 2 * i + j
                after(sync, q_ready, t + 1)
                sync.dma_start(dram["q_tab_t"][t, :, :], q_out[:, j, :]).then_inc(out_q[j], 16)
                after(sync, kv_ready, t + 1)
                sync.dma_start(dram["kv_tab_t"][t, :, :], kv_out[:, j, :]).then_inc(out_kv[j], 16)

            software_pipeline(sync, tiles, 2, [(0, load), (0, clear), (3, store)])
            sync.wait_ge(zeroed, 16 * (NREP + 1) * tiles)
            for j in range(2):
                sync.wait_ge(out_q[j], 16 * tiles // 2)
                sync.wait_ge(out_kv[j], 16 * tiles // 2)

        @block.vector
        def _(dve):
            def moments(i, j):
                t = 2 * i + j
                after(dve, x_in[j], 16 * i + 16)
                dve.bn_stats(stats[:, j, :], x[:, j, :]).then_inc(stats_ready, 1)
                dve.wait_ge(stats_ready, t + 1)
                held(dve, dve_passed)
                dve.bn_aggr(mv[:, j, :], stats[:, j, :]).then_inc(mv_ready, 1)
                dve.wait_ge(std_ready, t + 1)
                after(dve, h_ready, t - 1)
                dve.reciprocal(rstd[:, j, :], std[:, j, :]).then_inc(rstd_ready, 1)
                dve.wait_ge(rstd_ready, t + 1)
                dve.scalar_tensor_tensor(out=shift[:, j, :], in0=mv[:, j, 0:1], scalar=-1.0, in1=rstd[:, j, :],
                                         op0=ALU.mult, op1=ALU.mult).then_inc(shift_ready, 1)

            def add_bias(i, j):
                t = 2 * i + j
                dve.wait_ge(multiplied, t + 1)
                after(dve, out_q[j], 16 * i)
                dve.tensor_tensor(q_out[:, j, :], ps_q[j][:, :], w["bqkv"][:, 0:HD], ALU.add).then_inc(q_ready, 1)
                after(dve, out_kv[j], 16 * i)
                dve.tensor_tensor(kv_out[:, j, :], ps_kv[j][:, :], w["bqkv"][:, HD:3 * HD],
                                  ALU.add).then_inc(kv_ready, 1)

            software_pipeline(dve, tiles, 2, [(0, moments), (2, add_bias)])

        @block.scalar
        def _(act):
            def normalise(i, j):
                t = 2 * i + j
                act.wait_ge(mv_ready, t + 1)
                after(act, rstd_ready, t - 1)
                act.activation(std[:, j, :], mv[:, j, 1:2], ACT.Sqrt, bias=w["eps"][:, :]).then_inc(std_ready, 1)
                act.wait_ge(shift_ready, t + 1)
                after(act, turned, t - 1)
                after(act, xh_ready, t - 1)
                act.activation(h[:, j, :], x[:, j, :], ACT.Relu, bias=shift[:, j, :],
                               scale=rstd[:, j, :]).then_inc(h_ready, 1)

            def copy_turned(i, j):
                t = 2 * i + j
                act.wait_ge(turned, t + 1)
                after(act, multiplied, t - 1)
                act.copy(hT[:, j, :], ps_t[j][:, :]).then_inc(hT_ready, 1)

            software_pipeline(act, tiles, 2, [(0, normalise), (0, copy_turned)])

        @block.gpsimd
        def _(pool):
            def add_residual(i, j):
                t = 2 * i + j
                pool.wait_ge(h_ready, t + 1)
                pool.tensor_tensor(w["xh"][:, t, :], x[:, j, :], h[:, j, :], ALU.add).then_inc(xh_ready, 1)

            software_pipeline(pool, tiles, 2, [(0, add_residual)])

        @block.tensor
        def _(pe):
            def turn(i, j):
                t = 2 * i + j
                pe.wait_ge(h_ready, t + 1)
                after(pe, hT_ready, t - 1)
                for c in range(D // P):
                    last = pe.transpose(ps_t[j][:, c * P:(c + 1) * P], h[:, j, c * P:(c + 1) * P], w["ident"][:, :])
                last.then_inc(turned, 1)

            def multiply(i, j):
                t = 2 * i + j
                pe.wait_ge(hT_ready, t + 1)
                after(pe, q_ready, t - 1)
                after(pe, kv_ready, t - 1)
                for c in range(D // P):
                    pe.matmul(ps_q[j][:, :], hT[:, j, c * P:(c + 1) * P], w["wqkv"][:, c, 0:HD],
                              start=(c == 0), stop=(c == D // P - 1))
                for c in range(D // P):
                    last = pe.matmul(ps_kv[j][:, :], hT[:, j, c * P:(c + 1) * P], w["wqkv"][:, c, HD:3 * HD],
                                     start=(c == 0), stop=(c == D // P - 1))
                last.then_inc(multiplied, 1)

            software_pipeline(pe, tiles, 2, [(0, turn), (1, multiply)])


def build_attention(nc, w, dram, n_edges):
    tiles = n_edges // P
    G2 = 2 * U
    with ExitStack() as ctx:
        s = Space(nc, ctx, "at_")
        recv = s.sb("recv", [P, 2, U], I32)
        send = s.sb("send", [P, 2, U], I32)
        recv_row = s.sb("recv_row", [P, 2, U, P], I32)
        send_row = s.sb("send_row", [P, 2, U * P], I32)
        window = s.sb("window", [P, 2, 2 * HD])
        sent_by = s.sb("sent_by", [P, 2, U, P])
        q = s.sb("q", [P, 2, U, HD])
        kv = s.sb("kv", [P, 2, U, 2 * HD])
        prod = s.sb("prod", [P, U, HD])
        score = s.sb("score", [P, 2, U * H])
        m = s.sb("m", [P, 2, U, AW])
        same = s.sb("same", [P, 2, U, P])
        earlier = s.sb("earlier", [P, U, P])
        rank = s.sb("rank", [P, U])
        first = s.sb("first", [P, U])
        off = s.sb("off", [P, U])
        row_f = s.sb("row_f", [P, U])
        row = [[s.sb(f"row{b}{u}", [P, 1], I32) for u in range(U)] for b in range(2)]
        sums = s.sb("sums", [P, 2, U, AW])
        ps_kv = [s.ps(f"ps_kv{u}", [P, 2 * HD]) for u in range(U)]
        ps_sum = [s.ps(f"ps_sum{u}", [P, AW]) for u in range(U)]
        idx_in = [s.sem(f"idx_in{b}") for b in range(2)]
        window_in = [s.sem(f"window_in{b}") for b in range(2)]
        gathered = [s.sem(f"gathered{b}") for b in range(2)]
        scattered = [s.sem(f"scattered{r}") for r in range(NREP)]
        (sent_by_ready, spread, kv_ready, prod_ready, score_ready, same_ready, earlier_ready, rank_ready, first_ready,
         off_ready, row_f_ready, row_ready, exp_ready, msg_ready, summed, sums_ready, pool_passed,
         sync_passed) = (s.sem(n) for n in (
             "sent_by_ready", "spread", "kv_ready", "prod_ready", "score_ready", "same_ready", "earlier_ready",
             "rank_ready", "first_ready", "off_ready", "row_f_ready", "row_ready", "exp_ready", "msg_ready", "summed",
             "sums_ready", "pool_passed", "sync_passed"))
        block = ctx.enter_context(nc.Block())

        def scatters_done(eng, i, slot):
            r = slot % NREP
            if isinstance(i, int) and i < 0:
                return
            eng.wait_ge(scattered[r], 16 * ((G2 // NREP) * i + slot // NREP + 1))

        def sync_program(sync, windowed):
            def load(i, slot):
                if slot % U:
                    return
                b = slot // U
                g = 2 * i + b
                if windowed:
                    after(sync, spread, U * (g - 1))
                    held(sync, sync_passed)
                    first_node = sync.value_load(w["base"][0:1, bass.ds(g, 1)], min_val=0, max_val=w["last_base"])
                    sync.dma_start(window[:, b, :], dram["kv_tab"][bass.ds(first_node, P), :]).then_inc(window_in[b], 16)
                    after(sync, sent_by_ready, g - 1)
                    held(sync, sync_passed)
                    sync.dma_start(send_row[:, b, :],
                                   dram["dst_row"][g, :, :].to_broadcast([P, U * P])).then_inc(idx_in[b], 16)
                after(sync, gathered[b], (16 if windowed else 32) * U * i)
                held(sync, sync_passed)
                after(sync, row_f_ready, g - 1)
                held(sync, sync_passed)
                sync.dma_start(recv[:, b, :], dram["src_col"][g, :, :]).then_inc(idx_in[b], 16)
                sync.dma_start(recv_row[:, b, :, :].rearrange("p u j -> p (u j)"),
                               dram["src_row"][g, :, :].to_broadcast([P, U * P])).then_inc(idx_in[b], 16)
                if not windowed:
                    sync.dma_start(send[:, b, :], dram["dst_col"][g, :, :]).then_inc(idx_in[b], 16)

            software_pipeline(sync, tiles, G2, [(0, load)])

        def pool_program(pool, windowed):
            def gather(i, slot):
                b, u = slot // U, slot % U
                g = 2 * i + b
                if u == 0:
                    pool.wait_ge(idx_in[b], 48 * i + 48)
                    after(pool, msg_ready, g - 1)
                    held(pool, pool_passed)
                pool.indirect_dma_start(q[:, b, u, :], None, dram["q_tab"],
                                        bass.IndirectOffsetOnAxis(ap=recv[:, b, u:u + 1], axis=0)).then_inc(gathered[b], 16)
                if not windowed:
                    pool.indirect_dma_start(
                        kv[:, b, u, :], None, dram["kv_tab"],
                        bass.IndirectOffsetOnAxis(ap=send[:, b, u:u + 1], axis=0)).then_inc(gathered[b], 16)

            def scatter(i, slot):
                b, u = slot // U, slot % U
                r = slot % NREP
                k = G2 * i + slot
                pool.wait_ge(sums_ready, k + 1)
                after(pool, scattered[r], 16 * ((G2 // NREP) * i + slot // NREP))
                held(pool, pool_passed)
                pool.indirect_dma_start(dram["att_sum"][r], bass.IndirectOffsetOnAxis(ap=row[b][u][:, :], axis=0),
                                        sums[:, b, u, :], None, compute_op=ALU.add).then_inc(scattered[r], 16)

            software_pipeline(pool, tiles, G2, [(0, gather), (10, scatter)])
            for r in range(NREP):
                pool.wait_ge(scattered[r], 16 * tiles // NREP)

        def vector_program(dve, windowed):
            def senders(i, slot):
                if slot % U or not windowed:
                    return
                b = slot // U
                g = 2 * i + b
                dve.wait_ge(idx_in[b], 48 * i + 48)
                after(dve, spread, U * (g - 1))
                dve.tensor_scalar(sent_by[:, b, :, :].rearrange("p u e -> p (u e)"), send_row[:, b, :],
                                  w["node_of"][:, bass.ds(g, 1)], None, ALU.is_equal).then_inc(sent_by_ready, 1)

            def attend(i, slot):
                if slot % U:
                    return
                b = slot // U
                g = 2 * i + b
                dve.wait_ge(idx_in[b], 48 * i + 48)
                after(dve, summed, U * (g - 1))
                dve.tensor_tensor(same[:, b, :, :], recv_row[:, b, :, :],
                                  recv[:, b, :].unsqueeze(2).to_broadcast([P, U, P]), ALU.is_equal).then_inc(same_ready, 1)
                after(dve, row_ready, U * g)
                dve.tensor_scalar(off[:, :], recv[:, b, :], w["spare_f"][:, 0:1], None, ALU.subtract).then_inc(off_ready, 1)
                dve.wait_ge(same_ready, g + 1)
                dve.tensor_tensor(earlier[:, :, :], same[:, b, :, :],
                                  w["before"][:, :].unsqueeze(1).to_broadcast([P, U, P]), ALU.mult).then_inc(earlier_ready, 1)
                dve.wait_ge(earlier_ready, g + 1)
                dve.tensor_reduce(rank[:, :], earlier[:, :, :], AX.X, ALU.add).then_inc(rank_ready, 1)
                dve.wait_ge(gathered[b], (16 if windowed else 32) * U * (i + 1))
                if windowed:
                    dve.wait_ge(kv_ready, U * (g + 1))
                dve.tensor_tensor(prod[:, :, :], q[:, b, :, :], kv[:, b, :, 0:HD], ALU.mult).then_inc(prod_ready, 1)
                dve.wait_ge(rank_ready, g + 1)
                dve.tensor_scalar(first[:, :], rank[:, :], 0.0, None, ALU.is_equal).then_inc(first_ready, 1)
                dve.wait_ge(prod_ready, g + 1)
                after(dve, exp_ready, g - 1)
                dve.tensor_reduce(score[:, b, :], prod[:, :, :].rearrange("p u (h d) -> p (u h) d", h=H),
                                  AX.X, ALU.add).then_inc(score_ready, 1)
                dve.wait_ge(first_ready, g + 1)
                dve.wait_ge(off_ready, g + 1)
                dve.tensor_tensor(row_f[:, :], first[:, :], off[:, :], ALU.mult).then_inc(row_f_ready, 1)
                dve.wait_ge(row_f_ready, g + 1)
                for u in range(U):
                    scatters_done(dve, i - 1, U * b + u)
                    dve.tensor_scalar(row[b][u][:, :], row_f[:, u:u + 1], w["spare_f"][:, 0:1], None,
                                      ALU.add).then_inc(row_ready, 1)
                dve.wait_ge(exp_ready, g + 1)
                for u in range(U):
                    last = dve.tensor_tensor(
                        m[:, b, u, 0:HD].rearrange("p (h d) -> p h d", h=H),
                        kv[:, b, u, HD:2 * HD].rearrange("p (h d) -> p h d", h=H),
                        m[:, b, u, HD:AW].unsqueeze(2).to_broadcast([P, H, DK]), ALU.mult)
                last.then_inc(msg_ready, 1)

            software_pipeline(dve, tiles, G2, [(0, senders), (U, attend)])

        def scalar_program(act, windowed):
            def copy_kv(i, slot):
                if not windowed:
                    return
                b, u = slot // U, slot % U
                k = G2 * i + slot
                act.wait_ge(spread, k + 1)
                after(act, msg_ready, 2 * i + b - 1)
                act.copy(kv[:, b, u, :], ps_kv[u][:, :]).then_inc(kv_ready, 1)

            def exponentials(i, slot):
                if slot % U:
                    return
                b = slot // U
                g = 2 * i + b
                act.wait_ge(score_ready, g + 1)
                after(act, summed, U * (g - 1))
                act.activation(m[:, b, :, HD:AW], score[:, b, :].rearrange("p (u h) -> p u h", h=H),
                               ACT.Exp, scale=float(DK) ** -0.5).then_inc(exp_ready, 1)

            def copy_sums(i, slot):
                b, u = slot // U, slot % U
                k = G2 * i + slot
                act.wait_ge(summed, k + 1)
                scatters_done(act, i - 1, slot)
                act.copy(sums[:, b, u, :], ps_sum[u][:, :]).then_inc(sums_ready, 1)

            software_pipeline(act, tiles, G2, [(0, copy_kv), (U, exponentials), (G2, copy_sums)])

        def tensor_program(pe, windowed):
            def spread_kv(i, slot):
                if not windowed:
                    return
                b, u = slot // U, slot % U
                g = 2 * i + b
                k = G2 * i + slot
                if u == 0:
                    pe.wait_ge(window_in[b], 16 * (i + 1))
                    pe.wait_ge(sent_by_ready, g + 1)
                after(pe, kv_ready, k - U + 1)
                pe.matmul(ps_kv[u][:, :], sent_by[:, b, u, :], window[:, b, :], start=True, stop=True).then_inc(spread, 1)

            def add_up(i, slot):
                b, u = slot // U, slot % U
                g = 2 * i + b
                k = G2 * i + slot
                if u == 0:
                    pe.wait_ge(msg_ready, g + 1)
                    pe.wait_ge(same_ready, g + 1)
                after(pe, sums_ready, k - U + 1)
                pe.matmul(ps_sum[u][:, :], same[:, b, u, :], m[:, b, u, :], start=True, stop=True).then_inc(summed, 1)

            software_pipeline(pe, tiles, G2, [(0, spread_kv), (G2, add_up)])

        @block.sync
        def _(sync):
            by_path(sync, w["wide"], sync_program)

        @block.gpsimd
        def _(pool):
            by_path(pool, w["wide"], pool_program)

        @block.vector
        def _(dve):
            by_path(dve, w["wide"], vector_program)

        @block.scalar
        def _(act):
            by_path(act, w["wide"], scalar_program)

        @block.tensor
        def _(pe):
            by_path(pe, w["wide"], tensor_program)


def build_update(nc, w, dram, n_rows):
    tiles = n_rows // P
    with ExitStack() as ctx:
        s = Space(nc, ctx, "up_")
        part = s.sb("part", [P, 2, NREP, AW])
        tot = s.sb("tot", [P, 2, AW])
        empty = s.sb("empty", [P, 2, H])
        den = s.sb("den", [P, 2, H])
        rden = s.sb("rden", [P, 2, H])
        a = s.sb("a", [P, 2, HD])
        aT = s.sb("aT", [P, 2, 2, P])
        r1T = s.sb("r1T", [P, 2, 4, P])
        dense = s.sb("dense", [P, 2, D])
        h = s.sb("h", [P, 2, 4, MUL])
        hT = s.sb("hT", [P, 2, D])
        s_out = s.sb("s_out", [P, 2, D])
        stats = s.sb("stats", [P, 2, 6])
        mv = s.sb("mv", [P, 2, 2])
        std = s.sb("std", [P, 2, 1])
        rstd = s.sb("rstd", [P, 2, 1])
        shift = s.sb("shift", [P, 2, 1])
        ps_a = s.ps("ps_a", [P, HD])
        ps_1 = [s.ps(f"ps_1{j}", [P, 4 * P]) for j in range(2)]
        ps_2 = [s.ps(f"ps_2{j}", [P, D]) for j in range(2)]
        ps_h = s.ps("ps_h", [P, D])
        ps_s = [s.ps(f"ps_s{j}", [P, D]) for j in range(2)]
        part_in = [s.sem(f"part_in{j}") for j in range(2)]
        out_s = [s.sem(f"out_s{j}") for j in range(2)]
        names = ("tot_ready", "empty_ready", "den_ready", "rden_ready", "a_ready", "a_turned", "aT_ready", "multiplied1",
                 "r1T_ready", "multiplied2", "dense_ready", "x2_ready", "stats_ready", "mv_ready", "std_ready",
                 "rstd_ready", "shift_ready", "h_ready", "h_turned", "hT_ready", "multiplied3", "s_ready")
        (tot_ready, empty_ready, den_ready, rden_ready, a_ready, a_turned, aT_ready, multiplied1, r1T_ready,
         multiplied2, dense_ready, x2_ready, stats_ready, mv_ready, std_ready, rstd_ready, shift_ready, h_ready,
         h_turned, hT_ready, multiplied3, s_ready) = (s.sem(n) for n in names)
        dve_passed = s.sem("dve_passed")
        block = ctx.enter_context(nc.Block())

        @block.sync
        def _(sync):
            def load(i, j):
                t = 2 * i + j
                after(sync, tot_ready, t - 1)
                for r in range(NREP):
                    sync.dma_start(part[:, j, r, :], dram["att_sum_t"][r][t, :, :]).then_inc(part_in[j], 16)

            def store(i, j):
                t = 2 * i + j
                sync.wait_ge(s_ready, t + 1)
                sync.dma_start(dram["s_tab_t"][t, :, :], s_out[:, j, :]).then_inc(out_s[j], 16)

            software_pipeline(sync, tiles, 2, [(0, load), (6, store)])
            for j in range(2):
                sync.wait_ge(out_s[j], 16 * tiles // 2)

        @block.vector
        def _(dve):
            def normalise_sums(i, j):
                t = 2 * i + j
                dve.wait_ge(part_in[j], 16 * NREP * (i + 1))
                dve.tensor_tensor(tot[:, j, :], part[:, j, 0, :], part[:, j, 1, :], ALU.add).then_inc(tot_ready, 1)
                dve.wait_ge(tot_ready, t + 1)
                dve.tensor_scalar(empty[:, j, :], tot[:, j, HD:AW], 0.0, None, ALU.is_equal).then_inc(empty_ready, 1)
                dve.wait_ge(empty_ready, t + 1)
                dve.tensor_tensor(den[:, j, :], tot[:, j, HD:AW], empty[:, j, :], ALU.add).then_inc(den_ready, 1)
                dve.wait_ge(den_ready, t + 1)
                dve.reciprocal(rden[:, j, :], den[:, j, :]).then_inc(rden_ready, 1)
                dve.wait_ge(rden_ready, t + 1)
                after(dve, a_turned, t - 1)
                dve.scalar_tensor_tensor(out=a[:, j, :].rearrange("p (h d) -> p h d", h=H),
                                         in0=tot[:, j, 0:HD].rearrange("p (h d) -> p h d", h=H), scalar=0.0,
                                         in1=rden[:, j, :].unsqueeze(2).to_broadcast([P, H, DK]),
                                         op0=ALU.max, op1=ALU.mult).then_inc(a_ready, 1)

            def add_residual(i, j):
                t = 2 * i + j
                dve.wait_ge(multiplied2, t + 1)
                dve.tensor_tensor(dense[:, j, :], ps_2[j][:, :], w["bf"][:, :], ALU.add).then_inc(dense_ready, 1)
                dve.wait_ge(dense_ready, t + 1)
                dve.scalar_tensor_tensor(out=w["xh"][:, t, :], in0=dense[:, j, :], scalar=0.0, in1=w["xh"][:, t, :],
                                         op0=ALU.max, op1=ALU.add).then_inc(x2_ready, 1)
                dve.wait_ge(x2_ready, t + 1)
                held(dve, dve_passed)
                dve.bn_stats(stats[:, j, :], w["xh"][:, t, :]).then_inc(stats_ready, 1)
                dve.wait_ge(stats_ready, t + 1)
                held(dve, dve_passed)
                dve.bn_aggr(mv[:, j, :], stats[:, j, :]).then_inc(mv_ready, 1)
                dve.wait_ge(std_ready, t + 1)
                after(dve, h_ready, t - 1)
                dve.reciprocal(rstd[:, j, :], std[:, j, :]).then_inc(rstd_ready, 1)
                dve.wait_ge(rstd_ready, t + 1)
                dve.scalar_tensor_tensor(out=shift[:, j, :], in0=mv[:, j, 0:1], scalar=-1.0, in1=rstd[:, j, :],
                                         op0=ALU.mult, op1=ALU.mult).then_inc(shift_ready, 1)

            def copy_turned(i, j):
                t = 2 * i + j
                dve.wait_ge(h_turned, t + 1)
                after(dve, multiplied3, t - 1)
                dve.tensor_copy(hT[:, j, :], ps_h[:, :]).then_inc(hT_ready, 1)

            software_pipeline(dve, tiles, 2, [(0, normalise_sums), (2, add_residual), (3, copy_turned)])

        @block.scalar
        def _(act):
            def copy_aT(i, j):
                t = 2 * i + j
                act.wait_ge(a_turned, t + 1)
                after(act, multiplied1, t - 1)
                act.copy(aT[:, j, :, :].rearrange("p c n -> p (c n)"), ps_a[:, :]).then_inc(aT_ready, 1)

            def relu1(i, j):
                t = 2 * i + j
                act.wait_ge(multiplied1, t + 1)
                after(act, multiplied2, t - 1)
                for c in range(4):
                    act.activation(r1T[:, j, c, :], ps_1[j][:, c * P:(c + 1) * P], ACT.Relu,
                                   bias=w["ba"][:, c:c + 1]).then_inc(r1T_ready, 1)

            def norm(i, j):
                t = 2 * i + j
                act.wait_ge(mv_ready, t + 1)
                after(act, rstd_ready, t - 1)
                act.activation(std[:, j, :], mv[:, j, 1:2], ACT.Sqrt, bias=w["eps"][:, :]).then_inc(std_ready, 1)
                act.wait_ge(shift_ready, t + 1)
                after(act, h_turned, t - 1)
                act.activation(h[:, j, 0, :], w["xh"][:, t, 0:MUL], ACT.Relu, bias=shift[:, j, :],
                               scale=rstd[:, j, :]).then_inc(h_ready, 1)
                act.activation(h[:, j, 1:4, :], w["xh"][:, t, MUL:D].rearrange("p (u m) -> p m u", m=3), ACT.Relu,
                               bias=shift[:, j, :], scale=rstd[:, j, :]).then_inc(h_ready, 1)

            def copy_s(i, j):
                t = 2 * i + j
                act.wait_ge(multiplied3, t + 1)
                after(act, out_s[j], 16 * i)
                act.mul(s_out[:, j, :], ps_s[j][:, :], float(MUL) ** -0.5).then_inc(s_ready, 1)

            software_pipeline(act, tiles, 2, [(0, copy_aT), (1, relu1), (2, norm), (4, copy_s)])

        @block.tensor
        def _(pe):
            def turn_a(i, j):
                t = 2 * i + j
                pe.wait_ge(a_ready, t + 1)
                after(pe, aT_ready, t)
                for c in range(2):
                    last = pe.transpose(ps_a[:, c * P:(c + 1) * P], a[:, j, c * P:(c + 1) * P], w["ident"][:, :])
                last.then_inc(a_turned, 1)

            def layer1(i, j):
                t = 2 * i + j
                pe.wait_ge(aT_ready, t + 1)
                after(pe, r1T_ready, 4 * (t - 1))
                for o in range(4):
                    for c in range(2):
                        last = pe.matmul(ps_1[j][:, o * P:(o + 1) * P], w["wa"][:, c, o * P:(o + 1) * P], aT[:, j, c, :],
                                         start=(c == 0), stop=(c == 1))
                last.then_inc(multiplied1, 1)

            def layer2(i, j):
                t = 2 * i + j
                pe.wait_ge(r1T_ready, 4 * (t + 1))
                after(pe, dense_ready, t - 1)
                for c in range(4):
                    last = pe.matmul(ps_2[j][:, :], r1T[:, j, c, :], w["wf"][:, c, :], start=(c == 0), stop=(c == 3))
                last.then_inc(multiplied2, 1)

            def turn_h(i, j):
                t = 2 * i + j
                pe.wait_ge(h_ready, 2 * (t + 1))
                after(pe, hT_ready, t)
                for c in range(4):
                    last = pe.transpose(ps_h[:, c * P:(c + 1) * P], h[:, j, c, :], w["ident"][:, :])
                last.then_inc(h_turned, 1)

            def up(i, j):
                t = 2 * i + j
                pe.wait_ge(hT_ready, t + 1)
                after(pe, s_ready, t - 1)
                for c in range(4):
                    last = pe.matmul(ps_s[j][:, c * P:(c + 1) * P], hT[:, j, c * P:(c + 1) * P],
                                     w["wup"][:, min(c, 1), :], start=True, stop=True)
                last.then_inc(multiplied3, 1)

            software_pipeline(pe, tiles, 2, [(0, turn_a), (1, layer1), (2, layer2), (3, turn_h), (4, up)])


def build_messages(nc, w, dram, n_edges):
    tiles = n_edges // P
    G2 = 2 * U
    with ExitStack() as ctx:
        s = Space(nc, ctx, "ms_")
        send = s.sb("send", [P, 2, U], I32)
        recv = s.sb("recv", [P, 2, U], I32)
        recv_row = s.sb("recv_row", [P, 2, U, P], I32)
        y = s.sb("y", [P, 2, U, 4])
        radial = s.sb("radial", [2 * RB, 2, 2 * P])
        h1 = s.sb("h1", [P, 2 * P])
        h2 = s.sb("h2", [P, 2 * P])
        h3 = s.sb("h3", [P, 2, U * P])
        h3_parts = s.sb("h3_parts", [P, 2, U * P], F32R)
        node = s.sb("node", [P, G2, 4, MUL])
        to = s.sb("to", [P, 2, U, P])
        to_y = s.sb("to_y", [P, 2, U, 4, P])
        place = s.sb("place", [P, 2, U])
        earlier = s.sb("earlier", [P, U, P])
        rank = s.sb("rank", [P, U])
        first = s.sb("first", [P, U])
        off = s.sb("off", [P, U])
        row_f = s.sb("row_f", [P, U])
        row = [s.sb(f"row{n}", [P, 1], I32) for n in range(G2)]
        dot1 = s.sb("dot1", [P, MUL])
        dot2 = s.sb("dot2", [P, MUL])
        dot = s.sb("dot", [P, 2, MUL])
        prods = s.sb("prods", [P, 2, 6, MUL])
        sums = s.sb("sums", [P, 2, MW])
        ps_h = [s.ps(f"ps_h{n}", [P, U * P]) for n in range(2)]
        ps_w = [s.ps(f"ps_w{n}", [P, 4 * MUL]) for n in range(2)]
        ps_m = [s.ps(f"ps_m{n}", [P, MW]) for n in range(2)]
        idx_in = [s.sem(f"idx_in{b}") for b in range(2)]
        mlp_in = [s.sem(f"mlp_in{b}") for b in range(2)]
        gathered = [s.sem(f"gathered{n}") for n in range(G2)]
        names = ("scattered", "place_ready", "to_ready", "earlier_ready", "rank_ready", "first_ready", "off_ready",
                 "row_f_ready", "row_ready", "to_y_ready", "dot1_ready", "dot2_ready", "dot_ready", "prods_ready",
                 "hidden", "h1_ready", "h2_ready", "h3_ready", "high_ready", "parts_ready", "weighed", "summed",
                 "sums_ready", "pool_passed", "sync_passed")
        (scattered, place_ready, to_ready, earlier_ready, rank_ready, first_ready, off_ready,
         row_f_ready, row_ready, to_y_ready, dot1_ready, dot2_ready, dot_ready, prods_ready,
         hidden, h1_ready, h2_ready, h3_ready, high_ready, parts_ready, weighed, summed,
         sums_ready, pool_passed, sync_passed) = (s.sem(n) for n in names)
        block = ctx.enter_context(nc.Block())

        def sync_program(sync, windowed):
            def load(i, slot):
                if slot % U:
                    return
                b = slot // U
                g = 2 * i + b
                after(sync, hidden, 4 * (g - 1))
                held(sync, sync_passed)
                sync.dma_start(radial[:, b, :], dram["radial"][g, :, :]).then_inc(mlp_in[b], 16)
                if windowed:
                    after(sync, place_ready, g - 1)
                else:
                    after(sync, row_f_ready, g - 1)
                held(sync, sync_passed)
                after(sync, to_y_ready, 4 * U * (g - 1) if windowed else g - 1)
                held(sync, sync_passed)
                after(sync, dot_ready, U * (g - 1))
                held(sync, sync_passed)
                for u in range(U):
                    after(sync, gathered[U * b + u], 16 * i)
                sync.dma_start(send[:, b, :], dram["src_col"][g, :, :]).then_inc(idx_in[b], 16)
                sync.dma_start(recv[:, b, :], dram["dst_col"][g, :, :]).then_inc(idx_in[b], 16)
                sync.dma_start(y[:, b, :, :].rearrange("p u k -> p (u k)"), dram["y"][g, :, :]).then_inc(idx_in[b], 16)
                if not windowed:
                    sync.dma_start(recv_row[:, b, :, :].rearrange("p u j -> p (u j)"),
                                   dram["dst_row"][g, :, :].to_broadcast([P, U * P])).then_inc(idx_in[b], 16)

            software_pipeline(sync, tiles, G2, [(0, load)])

        def indices_in(eng, i, b, windowed):
            eng.wait_ge(idx_in[b], (48 if windowed else 64) * (i + 1))

        def pool_program(pool, windowed):
            def gather(i, slot):
                b, u = slot // U, slot % U
                k = G2 * i + slot
                if u == 0:
                    indices_in(pool, i, b, windowed)
                after(pool, prods_ready, k - G2 + 1)
                held(pool, pool_passed)
                pool.indirect_dma_start(node[:, slot, :, :].rearrange("p m c -> p (m c)"), None, dram["s_tab"],
                                        bass.IndirectOffsetOnAxis(ap=send[:, b, u:u + 1], axis=0)).then_inc(gathered[slot], 16)

            def add_to_rows(i, slot):
                k = G2 * i + slot
                pool.wait_ge(sums_ready, 2 * (k + 1))
                after(pool, scattered, 16 * k)
                held(pool, pool_passed)
                pool.indirect_dma_start(dram["msg_sum"], bass.IndirectOffsetOnAxis(ap=row[slot][:, :], axis=0),
                                        sums[:, slot % 2, :], None, compute_op=ALU.add).then_inc(scattered, 16)

            def add_to_window(i, slot):
                if slot % U != U - 1:
                    return
                b = slot // U
                g = 2 * i + b
                pool.wait_ge(sums_ready, 2 * (g + 1))
                after(pool, scattered, 16 * g)
                held(pool, pool_passed)
                first_node = pool.value_load(w["base"][0:1, bass.ds(g, 1)], min_val=0, max_val=w["last_base"])
                pool.dma_start(dram["msg_sum"][bass.ds(first_node, P), :], sums[:, b, :],
                               accum_op=ALU.add).then_inc(scattered, 16)

            if windowed:
                software_pipeline(pool, tiles, G2, [(0, gather), (G2, add_to_window)])
                pool.wait_ge(scattered, 16 * tiles // U)
            else:
                software_pipeline(pool, tiles, G2, [(0, gather), (5, add_to_rows)])
                pool.wait_ge(scattered, 16 * tiles)

        def vector_program(dve, windowed):
            def receivers(i, slot):
                if slot % U:
                    return
                b = slot // U
                g = 2 * i + b
                indices_in(dve, i, b, windowed)
                dve.tensor_scalar(place[:, b, :], recv[:, b, :], w["first_of"][:, bass.ds(g, 1)], None,
                                  ALU.subtract).then_inc(place_ready, 1)
                dve.wait_ge(place_ready, g + 1)
                after(dve, summed, U * (g - 1))
                after(dve, to_y_ready, 4 * U * (g - 1))
                dve.tensor_tensor(to[:, b, :, :], w["iota_f"][:, :].unsqueeze(1).to_broadcast([P, U, P]),
                                  place[:, b, :].unsqueeze(2).to_broadcast([P, U, P]), ALU.is_equal).then_inc(to_ready, 1)

            def shared_receivers(i, slot):
                if slot % U:
                    return
                b = slot // U
                g = 2 * i + b
                indices_in(dve, i, b, windowed)
                after(dve, summed, U * (g - 1))
                dve.tensor_tensor(to[:, b, :, :], recv_row[:, b, :, :],
                                  recv[:, b, :].unsqueeze(2).to_broadcast([P, U, P]), ALU.is_equal).then_inc(to_ready, 1)
                dve.wait_ge(to_ready, g + 1)
                dve.tensor_tensor(to_y[:, b, :, :, :], to[:, b, :, :].unsqueeze(2).to_broadcast([P, U, 4, P]),
                                  y[:, b, :, :].unsqueeze(3).to_broadcast([P, U, 4, P]), ALU.mult).then_inc(to_y_ready, 1)
                dve.tensor_tensor(earlier[:, :, :], to[:, b, :, :],
                                  w["before"][:, :].unsqueeze(1).to_broadcast([P, U, P]), ALU.mult).then_inc(earlier_ready, 1)
                dve.wait_ge(earlier_ready, g + 1)
                dve.tensor_reduce(rank[:, :], earlier[:, :, :], AX.X, ALU.add).then_inc(rank_ready, 1)
                after(dve, row_ready, U * g)
                dve.tensor_scalar(off[:, :], recv[:, b, :], w["spare_f"][:, 0:1], None, ALU.subtract).then_inc(off_ready, 1)
                dve.wait_ge(rank_ready, g + 1)
                dve.tensor_scalar(first[:, :], rank[:, :], 0.0, None, ALU.is_equal).then_inc(first_ready, 1)
                dve.wait_ge(first_ready, g + 1)
                dve.wait_ge(off_ready, g + 1)
                dve.tensor_tensor(row_f[:, :], first[:, :], off[:, :], ALU.mult).then_inc(row_f_ready, 1)
                dve.wait_ge(row_f_ready, g + 1)
                for u in range(U):
                    after(dve, scattered, 16 * (U * (g - 2) + u + 1))
                    dve.tensor_scalar(row[U * b + u][:, :], row_f[:, u:u + 1], w["spare_f"][:, 0:1], None,
                                      ALU.add).then_inc(row_ready, 1)

            def split_h3(i, slot):
                if slot % U:
                    return
                b = slot // U
                g = 2 * i + b
                dve.wait_ge(h3_ready, g + 1)
                after(dve, weighed, U * (g - 1))
                dve.tensor_copy(h3_parts[:, b, :], h3[:, b, :]).then_inc(high_ready, 1)
                dve.wait_ge(high_ready, g + 1)
                dve.tensor_tensor(h3_parts[HID:P, b, :], h3[HID:P, b, :], h3_parts[HID:P, b, :].bitcast(F32),
                                  ALU.subtract).then_inc(parts_ready, 1)

            def dots(i, slot):
                b, u, j = slot // U, slot % U, slot % 2
                k = G2 * i + slot
                dve.wait_ge(gathered[slot], 16 * (i + 1))
                after(dve, dot2_ready, k)
                dve.tensor_scalar(dot1[:, :], node[:, slot, 1, :], y[:, b, u, 1:2], None, ALU.mult).then_inc(dot1_ready, 1)
                dve.wait_ge(dot1_ready, k + 1)
                after(dve, dot_ready, k)
                dve.scalar_tensor_tensor(out=dot2[:, :], in0=node[:, slot, 2, :], scalar=y[:, b, u, 2:3], in1=dot1[:, :],
                                         op0=ALU.mult, op1=ALU.add).then_inc(dot2_ready, 1)
                dve.wait_ge(dot2_ready, k + 1)
                after(dve, prods_ready, k - 1)
                dve.scalar_tensor_tensor(out=dot[:, j, :], in0=node[:, slot, 3, :], scalar=y[:, b, u, 3:4], in1=dot2[:, :],
                                         op0=ALU.mult, op1=ALU.add).then_inc(dot_ready, 1)

            def products(i, slot):
                j = slot % 2
                k = G2 * i + slot
                dve.wait_ge(weighed, k + 1)
                after(dve, summed, k - 1)
                wts = ps_w[j][:, :].rearrange("p (w c) -> p w c", c=MUL)
                dve.tensor_tensor(prods[:, j, 0:5:4, :], wts[:, 0:2, :],
                                  node[:, slot, 0:1, :].to_broadcast([P, 2, MUL]), ALU.mult)
                dve.tensor_tensor(prods[:, j, 1:4, :], wts[:, 2:3, :].to_broadcast([P, 3, MUL]),
                                  node[:, slot, 1:4, :], ALU.mult)
                dve.wait_ge(dot_ready, k + 1)
                dve.tensor_tensor(prods[:, j, 5, :], wts[:, 3, :], dot[:, j, :], ALU.mult).then_inc(prods_ready, 1)

            if windowed:
                software_pipeline(dve, tiles, G2, [(2, receivers), (3, split_h3), (4, dots), (5, products)])
            else:
                software_pipeline(dve, tiles, G2, [(3, shared_receivers), (3, split_h3), (4, dots), (5, products)])

        def scalar_program(act, windowed):
            def silu(i, slot):
                layer, b = slot % U, slot // U
                g = 2 * i + b
                if layer == 3:
                    return
                n = 3 * b + layer
                act.wait_ge(hidden, 4 * g + (layer + 1 if layer < 2 else 4))
                if layer == 0:
                    act.activation(h1[:, :], ps_h[n % 2][:, 0:2 * P], ACT.Silu, scale=float(RB) ** -0.5).then_inc(h1_ready, 1)
                elif layer == 1:
                    act.activation(h2[:, :], ps_h[n % 2][:, 0:2 * P], ACT.Silu,
                                   scale=SILU_2MOM * float(HID) ** -0.5).then_inc(h2_ready, 1)
                else:
                    after(act, parts_ready, g - 1)
                    act.activation(h3[:, b, :], ps_h[n % 2][:, :], ACT.Silu,
                                   scale=SILU_2MOM * float(HID) ** -0.5).then_inc(h3_ready, 1)

            def times_y(i, slot):
                b, u = slot // U, slot % U
                g = 2 * i + b
                if u == 0:
                    act.wait_ge(to_ready, g + 1)
                    indices_in(act, i, b, windowed)
                    after(act, summed, U * (g - 1))
                for m in range(4):
                    act.mul(to_y[:, b, u, m, :], to[:, b, u, :], y[:, b, u, m:m + 1]).then_inc(to_y_ready, 1)

            def copy_group(i, slot):
                if slot % U != U - 1:
                    return
                b = slot // U
                g = 2 * i + b
                act.wait_ge(summed, U * (g + 1))
                after(act, scattered, 16 * (g - 1))
                for half in range(2):
                    act.copy(sums[:, b, half * D:(half + 1) * D],
                             ps_m[b][:, half * D:(half + 1) * D]).then_inc(sums_ready, 1)

            def copy_tile(i, slot):
                k = G2 * i + slot
                act.wait_ge(summed, k + 1)
                after(act, scattered, 16 * (k - 1))
                for half in range(2):
                    act.copy(sums[:, slot % 2, half * D:(half + 1) * D],
                             ps_m[slot % 2][:, half * D:(half + 1) * D]).then_inc(sums_ready, 1)

            if windowed:
                software_pipeline(act, tiles, G2, [(0, silu), (3, times_y), (6, copy_group)])
            else:
                software_pipeline(act, tiles, G2, [(0, silu), (6, copy_tile)])

        def tensor_program(pe, windowed):
            def mlp(i, slot):
                layer, b = slot % U, slot // U
                g = 2 * i + b
                if layer == 3:
                    return
                n = 3 * b + layer
                if layer == 0:
                    pe.wait_ge(mlp_in[b], 16 * (i + 1))
                    after(pe, h2_ready, g)
                    pe.matmul(ps_h[n % 2][:, 0:2 * P], w["mlp1"][:, :], radial[:, b, :],
                              start=True, stop=True).then_inc(hidden, 1)
                elif layer == 1:
                    pe.wait_ge(h1_ready, g + 1)
                    after(pe, h3_ready, g)
                    pe.matmul(ps_h[n % 2][:, 0:2 * P], w["mlp2"][:, :], h1[:, :], start=True, stop=True).then_inc(hidden, 1)
                else:
                    pe.wait_ge(h2_ready, g + 1)
                    for half in range(2):
                        pe.matmul(ps_h[n % 2][:, half * 2 * P:(half + 1) * 2 * P], w["mlp3"][:, half, :], h2[:, :],
                                  start=True, stop=True).then_inc(hidden, 1)

            def weigh(i, slot):
                b, u = slot // U, slot % U
                g = 2 * i + b
                k = G2 * i + slot
                if u == 0:
                    pe.wait_ge(parts_ready, g + 1)
                after(pe, prods_ready, k - 1)
                parts = h3_parts[:, b, u * P:(u + 1) * P]
                pe.matmul(ps_w[slot % 2][:, :], parts, w["mlp4_hi"][:, :], start=True, stop=False)
                pe.matmul(ps_w[slot % 2][:, :], parts, w["mlp4_lo"][:, :],
                          start=False, stop=True).then_inc(weighed, 1)

            def add_up(i, slot):
                b, u, j = slot // U, slot % U, slot % 2
                g = 2 * i + b
                k = G2 * i + slot
                if windowed:
                    pe.wait_ge(to_y_ready, 4 * (k + 1))
                elif u == 0:
                    pe.wait_ge(to_y_ready, g + 1)
                pe.wait_ge(prods_ready, k + 1)
                if windowed:
                    bank, opens, closes = ps_m[b], u == 0, u == U - 1
                    if u == 0:
                        after(pe, sums_ready, 2 * (g - 1))
                else:
                    bank, opens, closes = ps_m[j], True, True
                    after(pe, sums_ready, 2 * (k - 1))
                pe.matmul(bank[:, 0:4 * MUL], to_y[:, b, u, 0, :],
                          prods[:, j, 0:4, :].rearrange("p m c -> p (m c)"), start=opens, stop=closes)
                for m in range(3):
                    pe.matmul(bank[:, (4 + m) * MUL:(5 + m) * MUL], to_y[:, b, u, 1 + m, :], prods[:, j, 4, :],
                              start=opens and m == 0, stop=closes, skip_group_check=True)
                pe.matmul(bank[:, 7 * MUL:8 * MUL], to[:, b, u, :], prods[:, j, 5, :],
                          start=False, stop=closes, skip_group_check=True).then_inc(summed, 1)

            software_pipeline(pe, tiles, G2, [(0, mlp), (5, weigh), (6, add_up)])

        @block.sync
        def _(sync):
            by_path(sync, w["wide"], sync_program)

        @block.gpsimd
        def _(pool):
            by_path(pool, w["wide"], pool_program)

        @block.vector
        def _(dve):
            by_path(dve, w["wide"], vector_program)

        @block.scalar
        def _(act):
            by_path(act, w["wide"], scalar_program)

        @block.tensor
        def _(pe):
            by_path(pe, w["wide"], tensor_program)


def build_output(nc, w, dram, n_rows):
    tiles = n_rows // P
    TERMS = [((0, 0), (7, 1)), ((4, 2), (1, 3)), ((5, 2), (2, 3)), ((6, 2), (3, 3))]
    with ExitStack() as ctx:
        s = Space(nc, ctx, "ou_")
        tot = s.sb("tot", [P, 2, MW])
        totT = s.sb("totT", [P, 2, MW])
        out = s.sb("out", [P, 2, D])
        ps_t = [s.ps(f"ps_t{n}", [P, D]) for n in range(4)]
        ps_o = [s.ps(f"ps_o{j}", [P, D]) for j in range(2)]
        tot_in = [s.sem(f"tot_in{n}") for n in range(2)]
        stored = [s.sem(f"stored{j}") for j in range(2)]
        turned, totT_ready, multiplied, out_ready = (s.sem(n) for n in (
            "turned", "totT_ready", "multiplied", "out_ready"))
        dve_passed = s.sem("dve_passed")
        block = ctx.enter_context(nc.Block())

        @block.sync
        def _(sync):
            def load(i, j):
                t = 2 * i + j
                after(sync, turned, 2 * (t - 1))
                sync.dma_start(tot[:, j, :], dram["msg_sum_t"][t, :, :]).then_inc(tot_in[j], 16)

            def store(i, j):
                t = 2 * i + j
                sync.wait_ge(out_ready, 2 * (t + 1))
                sync.dma_start(dram["out_t"][t, :, :], out[:, j, :]).then_inc(stored[j], 16)

            software_pipeline(sync, tiles, 2, [(0, load), (4, store)])
            for j in range(2):
                sync.wait_ge(stored[j], 16 * tiles // 2)

        @block.vector
        def _(dve):
            def add_residual(i, j):
                t = 2 * i + j
                dve.wait_ge(multiplied, t + 1)
                after(dve, stored[j], 16 * i)
                dve.tensor_tensor(out[:, j, 0:MUL], ps_o[j][:, 0:MUL], w["xh"][:, t, 0:MUL], ALU.add).then_inc(out_ready, 1)
                dve.tensor_tensor(out[:, j, MUL:D].rearrange("p (v m) -> p m v", m=3),
                                  ps_o[j][:, MUL:D].rearrange("p (m v) -> p m v", m=3),
                                  w["xh"][:, t, MUL:D].rearrange("p (v m) -> p m v", m=3), ALU.add).then_inc(out_ready, 1)

            software_pipeline(dve, tiles, 2, [(0, add_residual)])

        @block.scalar
        def _(act):
            def copy_turned(i, j):
                t = 2 * i + j
                for half in range(2):
                    act.wait_ge(turned, 2 * t + half + 1)
                    after(act, multiplied, t - 1)
                    act.copy(totT[:, j, half * D:(half + 1) * D], ps_t[2 * j + half][:, :]).then_inc(totT_ready, 1)

            software_pipeline(act, tiles, 2, [(0, copy_turned)])

        @block.tensor
        def _(pe):
            def turn(i, j):
                t = 2 * i + j
                pe.wait_ge(tot_in[j], 16 * (i + 1))
                after(pe, totT_ready, 2 * (t - 1))
                for half in range(2):
                    for c in range(4):
                        last = pe.transpose(ps_t[2 * j + half][:, c * P:(c + 1) * P],
                                            tot[:, j, half * D + c * P:half * D + (c + 1) * P], w["ident"][:, :])
                    last.then_inc(turned, 1)

            def multiply(i, j):
                t = 2 * i + j
                pe.wait_ge(totT_ready, 2 * (t + 1))
                after(pe, out_ready, 2 * (t - 1))
                for n, terms in enumerate(TERMS):
                    for a, (block_of_row, weight) in enumerate(terms):
                        last = pe.matmul(ps_o[j][:, n * MUL:(n + 1) * MUL],
                                         totT[:, j, block_of_row * P:(block_of_row + 1) * P],
                                         w["wout"][:, weight, :], start=(a == 0), stop=(a == 1))
                last.then_inc(multiplied, 1)

            software_pipeline(pe, tiles, 2, [(0, turn), (1, multiply)])


def build(nc, dram, n_rows, n_edges):
    groups = n_edges // (U * P)

    def scratch(name, shape, dt=F32):
        return nc.dram_tensor(name, shape, dt, kind="Internal").ap()

    dram["q_tab"] = scratch("q_tab", (n_rows, HD))
    dram["kv_tab"] = scratch("kv_tab", (n_rows, 2 * HD))
    dram["s_tab"] = scratch("s_tab", (n_rows, D))
    dram["att_sum"] = [scratch(f"att_sum{r}", (n_rows, AW)) for r in range(NREP)]
    dram["msg_sum"] = scratch("msg_sum", (n_rows, MW))
    dram["base"] = scratch("base", (1, groups), I32)
    dram["span"] = scratch("span", (1, groups), I32)
    by_tile = "(t p) n -> t p n"
    for name in ("q_tab", "kv_tab", "s_tab", "msg_sum", "out"):
        dram[name + "_t"] = dram[name].rearrange(by_tile, p=P)
    dram["att_sum_t"] = [table.rearrange(by_tile, p=P) for table in dram["att_sum"]]

    with ExitStack() as ctx:
        s = Space(nc, ctx, "w_")
        w = {
            "xh": s.sb("xh", [P, n_rows // P, D]),
            "mlp1": s.sb("mlp1", [2 * RB, P]),
            "mlp2": s.sb("mlp2", [P, P]),
            "mlp3": s.sb("mlp3", [P, 2, P]),
            "mlp4_hi": s.sb("mlp4_hi", [P, 4 * MUL], F32R),
            "mlp4_lo": s.sb("mlp4_lo", [P, 4 * MUL], F32R),
            "wout": s.sb("wout", [P, 4, MUL]),
            "ident": s.sb("ident", [P, P]),
            "before": s.sb("before", [P, P]),
            "iota_f": s.sb("iota_f", [P, P]),
            "spare_f": s.sb("spare_f", [P, 1]),
            "base": s.sb("base", [P, groups], I32),
            "first_of": s.sb("first_of", [P, groups]),
            "node_of": s.sb("node_of", [P, groups]),
            "wide": s.sb("wide", [1, 1], I32),
            "last_base": n_rows - P,
        }
        with ExitStack() as first_layer:
            s = Space(nc, first_layer, "w_")
            w |= {
                "wa": s.sb("wa", [P, HD // P, D]),
                "ba": s.sb("ba", [P, D // P]),
                "wf": s.sb("wf", [P, D // P, D]),
                "bf": s.sb("bf", [P, D]),
                "wup": s.sb("wup", [P, 2, MUL]),
                "eps": s.sb("eps", [P, 1]),
            }
            with ExitStack() as projection:
                s = Space(nc, projection, "w_")
                w |= {
                    "wqkv": s.sb("wqkv", [P, D // P, 3 * HD]),
                    "bqkv": s.sb("bqkv", [P, 3 * HD]),
                    "zeros": s.sb("zeros", [P, MW]),
                }
                build_setup(nc, w, dram, n_rows, groups)
                build_project(nc, w, dram, n_rows)
            build_attention(nc, w, dram, n_edges)
            build_update(nc, w, dram, n_rows)
        build_messages(nc, w, dram, n_edges)
        build_output(nc, w, dram, n_rows)


WEIGHTS = ["L0_gnn_Wk", "L0_gnn_bk", "L0_gnn_Wq", "L0_gnn_bq", "L0_gnn_Wv", "L0_gnn_bv", "L0_gnn_Wa", "L0_gnn_ba",
           "L0_gnn_Wf", "L0_gnn_bf", "L1_gnn_W_up0", "L1_gnn_W_up1", "L1_gnn_W_mlp1", "L1_gnn_W_mlp2",
           "L1_gnn_W_mlp3", "L1_gnn_W_mlp4", "L1_gnn_W_out0", "L1_gnn_W_out1"]


def layout(inputs):
    import numpy as np

    x = np.asarray(inputs["x"])
    src, dst = np.asarray(inputs["src"]), np.asarray(inputs["dst"])
    n, e = x.shape[0], src.shape[0]
    n_rows, n_edges = node_rows(n), edge_rows(e)
    groups = n_edges // (U * P)
    arrays = {name: np.ascontiguousarray(inputs[name]) for name in WEIGHTS}
    xp = np.zeros((n_rows, D), x.dtype)
    xp[:n] = x
    arrays["x"] = xp.reshape(n_rows // P, P, D)
    for name, a in (("src", src), ("dst", dst)):
        full = np.full(n_edges, n, a.dtype)
        full[:e] = a
        arrays[name + "_row"] = full.reshape(groups, 1, U * P)
        arrays[name + "_col"] = np.ascontiguousarray(full.reshape(groups, U, P).transpose(0, 2, 1))
    y = np.asarray(inputs["edge_attr_4"])
    full = np.zeros((n_edges, 4), y.dtype)
    full[:e] = y
    arrays["y"] = np.ascontiguousarray(full.reshape(groups, U, P, 4).transpose(0, 2, 1, 3)).reshape(groups, P, U * 4)
    radial = np.asarray(inputs["edge_attr_8"])
    full = np.zeros((n_edges, RB), radial.dtype)
    full[:e] = radial
    arrays["radial"] = np.ascontiguousarray(
        full.reshape(groups, 2, 2 * P, RB).transpose(0, 1, 3, 2)).reshape(groups, 2 * RB, 2 * P)
    return arrays, n_rows, n_edges


def kernel(**inputs):
    import numpy as np
    import concourse.bacc as bacc
    from concourse.bass_utils import run_bass_kernel_spmd

    arrays, n_rows, n_edges = layout(inputs)
    nc = bacc.Bacc("TRN2", target_bir_lowering=False, num_devices=1)
    dram, by_name = {}, {}
    for name, a in arrays.items():
        by_name[f"in_{name}"] = a
        dram[name] = nc.dram_tensor(f"in_{name}", a.shape, mybir.dt.from_np(a.dtype), kind="ExternalInput").ap()
    dram["out"] = nc.dram_tensor("out", (n_rows, D), F32, kind="ExternalOutput").ap()
    build(nc, dram, n_rows, n_edges)
    result = run_bass_kernel_spmd(nc, [by_name], core_ids=[0])
    return result.results[0]["out"][:np.asarray(inputs["x"]).shape[0]]
```

```python
from contextlib import ExitStack

import concourse.bass as bass
from concourse import mybir

ALU = mybir.AluOpType
ACT = mybir.ActivationFunctionType
AX = mybir.AxisListType
F32 = mybir.dt.float32
F32R = mybir.dt.float32r
BF16 = mybir.dt.bfloat16
I32 = mybir.dt.int32

P = 128
D = 512
H, DK = 8, 32
HD = H * DK
AW = HD + H
MUL = 128
HID = 64
RB = 8
MW = 8 * MUL
U = 4
SPAN = 32
NREP = 2
EPS = 1e-5
SILU_2MOM = 1.679177


def node_rows(n):
    full = -(-n // P) * P + P
    return -(-full // (2 * P)) * 2 * P


def edge_rows(n):
    return -(-n // (2 * U * P)) * 2 * U * P


def after(eng, sem, value):
    if not isinstance(value, int) or value > 0:
        eng.wait_ge(sem, value)


def held(eng, passed):
    eng.sem_inc(passed, 1)


def software_pipeline(eng, tiles, unroll, stages):
    rounds = tiles // unroll
    assert rounds > -(-max(lag for lag, _ in stages) // unroll)
    start = 1 + -(-max(lag for lag, _ in stages) // unroll)
    for t in range(start * unroll):
        for lag, stage in stages:
            if t >= lag:
                stage((t - lag) // unroll, (t - lag) % unroll)
    with eng.Fori(start, rounds) as i:
        for j in range(unroll):
            for lag, stage in stages:
                back = (j - lag) // unroll
                stage(i + back if back else i, (j - lag) % unroll)
    for t in range(rounds * unroll, tiles + max(lag for lag, _ in stages)):
        for lag, stage in stages:
            if t - lag < tiles:
                stage((t - lag) // unroll, (t - lag) % unroll)


def by_path(eng, wide, program):
    flag = eng.value_load(wide[0:1, 0:1], min_val=0, max_val=1)
    with eng.If(flag > 0):
        program(eng, False)
    with eng.Else():
        program(eng, True)


class Space:

    def __init__(self, nc, ctx, prefix):
        self.nc, self.ctx, self.prefix = nc, ctx, prefix

    def sb(self, name, shape, dt=F32):
        return self.ctx.enter_context(self.nc.sbuf_tensor(self.prefix + name, shape, dt))

    def ps(self, name, shape):
        return self.ctx.enter_context(self.nc.psum_tensor(self.prefix + name, shape, F32))

    def sem(self, name):
        return self.ctx.enter_context(self.nc.semaphore(self.prefix + name))


def build_setup(nc, w, dram, n_rows, groups):
    half_groups = groups // 2
    with ExitStack() as ctx:
        s = Space(nc, ctx, "su_")
        mlp4 = s.sb("mlp4", [P, 4 * MUL])
        wout = s.sb("wout", [P, 4, MUL])
        wqkv = s.sb("wqkv", [P, D // P, 3 * HD])
        send = s.sb("send", [half_groups, 2, U * P], I32)
        least = s.sb("least", [half_groups, 2, U])
        most = s.sb("most", [half_groups, 2, U])
        base = s.sb("base", [half_groups, 2])
        base_i = s.sb("base_i", [half_groups, 2], I32)
        from_base = s.sb("from_base", [half_groups, 2, U])
        offset = s.sb("offset", [half_groups, 2, U])
        offset_i = s.sb("offset_i", [half_groups, 2, U], I32)
        start = s.sb("start", [half_groups, 2, U])
        span_i = s.sb("span_i", [half_groups, 2, U], I32)
        spans = s.sb("spans", [1, groups * U], I32)
        widest = s.sb("widest", [1, 1])
        base_f = s.sb("base_f", [P, groups])
        iota_i = s.sb("iota_i", [P, P], I32)
        part_i = s.sb("part_i", [P, 1], I32)
        part_f = s.sb("part_f", [P, 1])
        spare_i = s.sb("spare_i", [P, 1], I32)
        (loaded, cleared, made, send_in, tiles_ready, base_ready, base_i_ready, from_base_ready, offset_ready,
         offset_i_ready, start_ready, span_ready, base_out, base_in, widest_ready, window_ready,
         split) = (s.sem(n) for n in (
             "loaded", "cleared", "made", "send_in", "tiles_ready", "base_ready", "base_i_ready", "from_base_ready",
             "offset_ready", "offset_i_ready", "start_ready", "span_ready", "base_out", "base_in", "widest_ready",
             "window_ready", "split"))
        block = ctx.enter_context(nc.Block())
        N_LOADED = 3 + 3 + 4 + 2 + 2 + 2 + 4 + 4

        @block.sync
        def _(sync):
            sync.dma_start(send[:, :, :], dram["dst_row"].rearrange("(p c) a e -> p (c a) e", c=2)).then_inc(send_in, 16)
            for t, name in enumerate(("L0_gnn_Wq", "L0_gnn_Wk", "L0_gnn_Wv")):
                sync.dma_start(wqkv[:, :, t * HD:(t + 1) * HD],
                               dram[name].rearrange("(c p) n -> p c n", p=P)).then_inc(loaded, 16)
            for t, name in enumerate(("L0_gnn_bq", "L0_gnn_bk", "L0_gnn_bv")):
                sync.dma_start(w["bqkv"][:, t * HD:(t + 1) * HD],
                               dram[name].rearrange("(a n) -> a n", a=1).to_broadcast([P, HD])).then_inc(loaded, 16)
            sync.dma_start(w["bf"][:, :],
                           dram["L0_gnn_bf"].rearrange("(a n) -> a n", a=1).to_broadcast([P, D])).then_inc(loaded, 16)
            sync.dma_start(w["ba"][:, :], dram["L0_gnn_ba"].rearrange("(c p) -> p c", p=P),
                           allow_slow_non_contiguous=True).then_inc(loaded, 16)
            sync.dma_start(w["wa"][:, :, :], dram["L0_gnn_Wa"].rearrange("(c p) n -> p c n", p=P)).then_inc(loaded, 16)
            sync.dma_start(w["wf"][:, :, :], dram["L0_gnn_Wf"].rearrange("(c p) n -> p c n", p=P)).then_inc(loaded, 16)
            sync.wait_ge(base_i_ready, 1)
            sync.dma_start(dram["base"].rearrange("a (p c) -> (a p) c", c=2), base_i[:, :]).then_inc(base_out, 16)
            for name, tile, ready in (("offset", offset_i, offset_i_ready), ("start", start, start_ready),
                                      ("span", span_i, span_ready)):
                sync.wait_ge(ready, 1)
                sync.dma_start(dram[name].rearrange("a (p c) -> (a p) c", c=2 * U),
                               tile[:, :, :].rearrange("p c u -> p (c u)")).then_inc(base_out, 16)
            sync.wait_ge(base_out, 64)
            sync.dma_start(w["base"][:, :], dram["base"].to_broadcast([P, groups])).then_inc(base_in, 16)
            sync.dma_start(w["start"][:, :], dram["start"].to_broadcast([P, groups * U])).then_inc(base_in, 16)
            sync.dma_start(w["offset"][:, :], dram["offset"]).then_inc(base_in, 16)
            sync.dma_start(spans[:, :], dram["span"]).then_inc(base_in, 16)

        @block.scalar
        def _(act):
            act.dma_start(w["wup"][:, 0, :], dram["L1_gnn_W_up0"]).then_inc(loaded, 16)
            act.dma_start(w["wup"][:, 1, :], dram["L1_gnn_W_up1"]).then_inc(loaded, 16)
            act.dma_start(wout[:, 0:2, :], dram["L1_gnn_W_out0"].rearrange("(c p) n -> p c n", p=P)).then_inc(loaded, 16)
            act.dma_start(wout[:, 2:4, :], dram["L1_gnn_W_out1"].rearrange("(c p) n -> p c n", p=P)).then_inc(loaded, 16)
            act.wait_ge(cleared, 3)
            for half in range(2):
                lo, hi = half * HID, (half + 1) * HID
                act.dma_start(mlp4[lo:hi, :], dram["L1_gnn_W_mlp4"]).then_inc(loaded, 16)
                act.dma_start(w["mlp1"][half * RB:(half + 1) * RB, lo:hi], dram["L1_gnn_W_mlp1"]).then_inc(loaded, 16)
                act.dma_start(w["mlp2"][lo:hi, lo:hi], dram["L1_gnn_W_mlp2"]).then_inc(loaded, 16)
                for copy in range(2):
                    act.dma_start(w["mlp3"][lo:hi, half, copy * HID:(copy + 1) * HID], dram["L1_gnn_W_mlp3"]).then_inc(loaded, 16)
            act.wait_ge(loaded, 16 * N_LOADED)

        @block.gpsimd
        def _(pool):
            pool.memset(w["mlp1"][:, :], 0.0).then_inc(cleared, 1)
            pool.memset(w["mlp2"][:, :], 0.0).then_inc(cleared, 1)
            pool.memset(w["mlp3"][:, :, :], 0.0).then_inc(cleared, 1)
            pool.memset(w["ident"][:, :], 0.0).then_inc(made, 1)
            pool.memset(w["before"][:, :], 1.0).then_inc(made, 1)
            pool.memset(w["zeros"][:, :], 0.0).then_inc(made, 1)
            pool.wait_ge(made, 3)
            pool.affine_select(out=w["ident"][:, :], in_=w["ident"][:, :], compare_op=ALU.not_equal, fill=1.0,
                               base=0, pattern=[[-1, P]], channel_multiplier=1).then_inc(made, 1)
            pool.affine_select(out=w["before"][:, :], in_=w["before"][:, :], compare_op=ALU.is_gt, fill=0.0,
                               base=0, pattern=[[-1, P]], channel_multiplier=1).then_inc(made, 1)
            pool.iota(spare_i[:, :], pattern=[[0, 1]], base=n_rows - P, channel_multiplier=1).then_inc(made, 1)
            pool.iota(iota_i[:, :], pattern=[[1, P]], base=0, channel_multiplier=0).then_inc(made, 1)
            pool.iota(part_i[:, :], pattern=[[0, 1]], base=0, channel_multiplier=1).then_inc(made, 1)

        @block.vector
        def _(dve):
            dve.memset(w["eps"][:, :], EPS)
            dve.wait_ge(send_in, 16)
            by_tile = send[:, :, :].rearrange("p c (u e) -> p c u e", u=U)
            dve.tensor_reduce(least[:, :, :], by_tile, AX.X, ALU.min).then_inc(tiles_ready, 1)
            dve.tensor_reduce(most[:, :, :], by_tile, AX.X, ALU.max).then_inc(tiles_ready, 1)
            dve.wait_ge(tiles_ready, 2)
            dve.tensor_reduce(base[:, :], least[:, :, :], AX.X, ALU.min).then_inc(base_ready, 1)
            dve.wait_ge(base_ready, 1)
            dve.tensor_copy(base_i[:, :], base[:, :]).then_inc(base_i_ready, 1)
            group_base = base[:, :].unsqueeze(2).to_broadcast([half_groups, 2, U])
            dve.tensor_tensor(from_base[:, :, :], least[:, :, :], group_base, ALU.subtract).then_inc(from_base_ready, 1)
            dve.wait_ge(from_base_ready, 1)
            dve.tensor_scalar(offset[:, :, :], from_base[:, :, :], float(P - SPAN), None, ALU.min).then_inc(offset_ready, 1)
            dve.wait_ge(offset_ready, 1)
            dve.tensor_copy(offset_i[:, :, :], offset[:, :, :]).then_inc(offset_i_ready, 1)
            dve.tensor_tensor(start[:, :, :], offset[:, :, :], group_base, ALU.add).then_inc(start_ready, 1)
            dve.wait_ge(start_ready, 1)
            dve.tensor_tensor(span_i[:, :, :], most[:, :, :], start[:, :, :], ALU.subtract).then_inc(span_ready, 1)
            dve.wait_ge(made, 8)
            dve.tensor_copy(w["spare_f"][:, :], spare_i[:, :])
            dve.tensor_copy(w["iota_f"][:, :], iota_i[:, :])
            dve.tensor_copy(part_f[:, :], part_i[:, :]).then_inc(window_ready, 1)
            dve.memset(w["zero"][:, :], 0.0)
            dve.wait_ge(base_in, 64)
            dve.tensor_copy(base_f[:, :], w["base"][:, :]).then_inc(window_ready, 1)
            dve.tensor_reduce(widest[:, :], spans[:, :], AX.X, ALU.max).then_inc(widest_ready, 1)
            dve.wait_ge(window_ready, 2)
            dve.tensor_scalar(w["node_of"][:, :], base_f[:, :], part_f[:, 0:1], None, ALU.add).then_inc(window_ready, 1)
            dve.wait_ge(widest_ready, 1)
            dve.tensor_scalar(w["wide"][:, :], widest[:, :], float(SPAN), None, ALU.is_ge)
            dve.wait_ge(loaded, 16 * N_LOADED)
            dve.tensor_copy(w["mlp4_hi"][:, :], mlp4[:, :]).then_inc(split, 1)
            dve.tensor_copy(w["wqkv_hi"][:, :, :], wqkv[:, :, :]).then_inc(split, 1)
            dve.wait_ge(split, 2)
            dve.tensor_tensor(w["wqkv_lo"][:, :, :], wqkv[:, :, :], w["wqkv_hi"][:, :, :].bitcast(F32), ALU.subtract)
            dve.tensor_tensor(w["mlp4_lo"][:, :], mlp4[:, :], w["mlp4_hi"][:, :].bitcast(F32), ALU.subtract)
            k = (SILU_2MOM / HID ** 0.5) / (2 * MUL) ** 0.5 / 10.0
            for c, factor in enumerate((k, k / 3.0 ** 0.5, k, k)):
                dve.tensor_scalar(w["wout"][:, c, :], wout[:, c, :], factor, None, ALU.mult)


def build_project(nc, w, dram, n_rows):
    tiles = n_rows // P
    with ExitStack() as ctx:
        s = Space(nc, ctx, "pj_")
        x = s.sb("x", [P, 4, D])
        h = s.sb("h", [P, 2, D])
        hT_hi = s.sb("hT_hi", [P, 2, D], F32R)
        hT_lo = s.sb("hT_lo", [P, 2, D], F32R)
        q_out = s.sb("q_out", [P, 2, HD])
        kv_out = s.sb("kv_out", [P, 2, 2 * HD])
        stats = s.sb("stats", [P, 2, 6])
        mv = s.sb("mv", [P, 2, 2])
        std = s.sb("std", [P, 2, 1])
        rstd = s.sb("rstd", [P, 2, 1])
        shift = s.sb("shift", [P, 2, 1])
        ps_t = [s.ps(f"ps_t{j}", [P, D]) for j in range(2)]
        ps_q = [s.ps(f"ps_q{j}", [P, HD]) for j in range(2)]
        ps_kv = [s.ps(f"ps_kv{j}", [P, 2 * HD]) for j in range(2)]
        x_in = [s.sem(f"x_in{n}") for n in range(4)]
        out_q = [s.sem(f"out_q{j}") for j in range(2)]
        out_kv = [s.sem(f"out_kv{j}") for j in range(2)]
        zeroed = s.sem("zeroed")
        (stats_ready, mv_ready, std_ready, rstd_ready, shift_ready, h_ready, xh_ready, turned, hi_ready, lo_ready,
         multiplied, q_ready, kv_ready) = (s.sem(n) for n in (
             "stats_ready", "mv_ready", "std_ready", "rstd_ready", "shift_ready", "h_ready", "xh_ready", "turned",
             "hi_ready", "lo_ready", "multiplied", "q_ready", "kv_ready"))
        dve_passed = s.sem("dve_passed")
        block = ctx.enter_context(nc.Block())

        @block.sync
        def _(sync):
            def load(i, n):
                t, j = 4 * i + n, n % 2
                after(sync, xh_ready, t - 3)
                sync.dma_start(x[:, n, :], dram["x"][t, :, :]).then_inc(x_in[n], 16)

            def clear(i, n):
                t, j = 4 * i + n, n % 2
                for table in dram["att_sum_t"]:
                    sync.dma_start(table[t, :, :], w["zeros"][:, 0:AW]).then_inc(zeroed, 16)
                sync.dma_start(dram["msg_rows_t"][t, :, :], w["zeros"][:, :]).then_inc(zeroed, 16)

            def store(i, n):
                t, j = 4 * i + n, n % 2
                after(sync, q_ready, t + 1)
                sync.dma_start(dram["q_tab_t"][t, :, :], q_out[:, j, :]).then_inc(out_q[j], 16)
                after(sync, kv_ready, t + 1)
                sync.dma_start(dram["kv_tab_t"][t, :, :], kv_out[:, j, :]).then_inc(out_kv[j], 16)

            software_pipeline(sync, tiles, 4, [(0, load), (0, clear), (7, store)])
            sync.wait_ge(zeroed, 16 * (NREP + 1) * tiles)
            for j in range(2):
                sync.wait_ge(out_q[j], 16 * tiles // 2)
                sync.wait_ge(out_kv[j], 16 * tiles // 2)

        @block.vector
        def _(dve):
            def moments(i, n):
                t, j = 4 * i + n, n % 2
                after(dve, x_in[n], 16 * i + 16)
                dve.bn_stats(stats[:, j, :], x[:, n, :]).then_inc(stats_ready, 1)
                dve.wait_ge(stats_ready, t + 1)
                held(dve, dve_passed)
                after(dve, std_ready, t - 1)
                held(dve, dve_passed)
                dve.bn_aggr(mv[:, j, :], stats[:, j, :]).then_inc(mv_ready, 1)

            def scales(i, n):
                t, j = 4 * i + n, n % 2
                dve.wait_ge(std_ready, t + 1)
                after(dve, h_ready, t - 1)
                dve.reciprocal(rstd[:, j, :], std[:, j, :]).then_inc(rstd_ready, 1)
                dve.wait_ge(rstd_ready, t + 1)
                dve.scalar_tensor_tensor(out=shift[:, j, :], in0=mv[:, j, 0:1], scalar=-1.0, in1=rstd[:, j, :],
                                         op0=ALU.mult, op1=ALU.mult).then_inc(shift_ready, 1)

            def subtract_high(i, n):
                t, j = 4 * i + n, n % 2
                dve.wait_ge(hi_ready, t + 1)
                after(dve, multiplied, t - 1)
                dve.tensor_tensor(hT_lo[:, j, :], ps_t[j][:, :], hT_hi[:, j, :].bitcast(F32),
                                  ALU.subtract).then_inc(lo_ready, 1)

            def add_bias(i, n):
                t, j = 4 * i + n, n % 2
                dve.wait_ge(multiplied, t + 1)
                after(dve, out_q[j], 16 * (2 * i + n // 2))
                dve.tensor_tensor(q_out[:, j, :], ps_q[j][:, :], w["bqkv"][:, 0:HD], ALU.add).then_inc(q_ready, 1)
                after(dve, out_kv[j], 16 * (2 * i + n // 2))
                dve.tensor_tensor(kv_out[:, j, :], ps_kv[j][:, :], w["bqkv"][:, HD:3 * HD],
                                  ALU.add).then_inc(kv_ready, 1)

            software_pipeline(dve, tiles, 4, [(1, scales), (4, subtract_high), (6, add_bias), (0, moments)])

        @block.scalar
        def _(act):
            def deviation(i, n):
                t, j = 4 * i + n, n % 2
                act.wait_ge(mv_ready, t + 1)
                after(act, rstd_ready, t - 1)
                act.activation(std[:, j, :], mv[:, j, 1:2], ACT.Sqrt, bias=w["eps"][:, :]).then_inc(std_ready, 1)

            def normalise(i, n):
                t, j = 4 * i + n, n % 2
                act.wait_ge(shift_ready, t + 1)
                after(act, turned, t - 1)
                after(act, xh_ready, t - 1)
                act.activation(h[:, j, :], x[:, n, :], ACT.Relu, bias=shift[:, j, :],
                               scale=rstd[:, j, :]).then_inc(h_ready, 1)

            def copy_turned(i, n):
                t, j = 4 * i + n, n % 2
                act.wait_ge(turned, t + 1)
                after(act, multiplied, t - 1)
                act.copy(hT_hi[:, j, :], ps_t[j][:, :]).then_inc(hi_ready, 1)

            software_pipeline(act, tiles, 4, [(1, deviation), (4, copy_turned), (2, normalise)])

        @block.gpsimd
        def _(pool):
            def add_residual(i, n):
                t, j = 4 * i + n, n % 2
                pool.wait_ge(h_ready, t + 1)
                pool.tensor_tensor(w["xh"][:, t, :], x[:, n, :], h[:, j, :], ALU.add).then_inc(xh_ready, 1)

            software_pipeline(pool, tiles, 4, [(0, add_residual)])

        @block.tensor
        def _(pe):
            def turn(i, n):
                t, j = 4 * i + n, n % 2
                pe.wait_ge(h_ready, t + 1)
                after(pe, lo_ready, t - 1)
                for c in range(D // P):
                    last = pe.transpose(ps_t[j][:, c * P:(c + 1) * P], h[:, j, c * P:(c + 1) * P], w["ident"][:, :])
                last.then_inc(turned, 1)

            def multiply(i, n):
                t, j = 4 * i + n, n % 2
                pe.wait_ge(lo_ready, t + 1)
                after(pe, q_ready, t - 1)
                after(pe, kv_ready, t - 1)
                for out, lo, hi in ((ps_q[j], 0, HD), (ps_kv[j], HD, 3 * HD)):
                    for c in range(D // P):
                        high, low = (part[:, j, c * P:(c + 1) * P] for part in (hT_hi, hT_lo))
                        w_high, w_low = (w[part][:, c, lo:hi] for part in ("wqkv_hi", "wqkv_lo"))
                        pe.matmul(out[:, :], high, w_high, start=(c == 0), stop=False)
                        pe.matmul(out[:, :], high, w_low, start=False, stop=False)
                        last = pe.matmul(out[:, :], low, w_high, start=False, stop=(c == D // P - 1))
                last.then_inc(multiplied, 1)

            software_pipeline(pe, tiles, 4, [(5, multiply), (3, turn)])


def build_attention(nc, w, dram, n_edges):
    tiles = n_edges // P
    G2 = 2 * U
    with ExitStack() as ctx:
        s = Space(nc, ctx, "at_")
        recv = s.sb("recv", [P, 2, U], I32)
        send = s.sb("send", [P, 2, U], I32)
        recv_row = s.sb("recv_row", [P, 2, U, P], I32)
        send_row = s.sb("send_row", [P, 2, U * P], I32)
        window = s.sb("window", [P, 2, 2 * HD])
        sent_by = s.sb("sent_by", [P, 2, U, P])
        q = s.sb("q", [P, 2, U, HD])
        kv = s.sb("kv", [P, 2, U, 2 * HD])
        prod = s.sb("prod", [P, U, HD])
        score = s.sb("score", [P, 2, U * H])
        m = s.sb("m", [P, 2, U, AW])
        same = s.sb("same", [P, 2, U, P])
        earlier = s.sb("earlier", [P, U, P])
        rank = s.sb("rank", [P, U])
        first = s.sb("first", [P, U])
        off = s.sb("off", [P, U])
        row_f = s.sb("row_f", [P, U])
        row = [[s.sb(f"row{b}{u}", [P, 1], I32) for u in range(U)] for b in range(2)]
        sums = s.sb("sums", [P, 2, U, AW])
        ps_kv = [s.ps(f"ps_kv{u}", [P, 2 * HD]) for u in range(U)]
        ps_sum = [s.ps(f"ps_sum{u}", [P, AW]) for u in range(U)]
        idx_in = [s.sem(f"idx_in{b}") for b in range(2)]
        window_in = [s.sem(f"window_in{b}") for b in range(2)]
        gathered = [s.sem(f"gathered{b}") for b in range(2)]
        scattered = [s.sem(f"scattered{r}") for r in range(NREP)]
        (sent_by_ready, spread, kv_ready, prod_ready, score_ready, same_ready, earlier_ready, rank_ready, first_ready,
         off_ready, row_f_ready, row_ready, exp_ready, msg_ready, summed, sums_ready, pool_passed,
         sync_passed) = (s.sem(n) for n in (
             "sent_by_ready", "spread", "kv_ready", "prod_ready", "score_ready", "same_ready", "earlier_ready",
             "rank_ready", "first_ready", "off_ready", "row_f_ready", "row_ready", "exp_ready", "msg_ready", "summed",
             "sums_ready", "pool_passed", "sync_passed"))
        block = ctx.enter_context(nc.Block())

        def scatters_done(eng, i, slot):
            r = slot % NREP
            if isinstance(i, int) and i < 0:
                return
            eng.wait_ge(scattered[r], 16 * ((G2 // NREP) * i + slot // NREP + 1))

        def sync_program(sync, windowed):
            def load(i, slot):
                if slot % U:
                    return
                b = slot // U
                g = 2 * i + b
                if windowed:
                    after(sync, spread, U * (g - 1))
                    held(sync, sync_passed)
                    first_node = sync.value_load(w["base"][0:1, bass.ds(g, 1)], min_val=0, max_val=w["last_base"])
                    sync.dma_start(window[:, b, :], dram["kv_tab"][bass.ds(first_node, P), :]).then_inc(window_in[b], 16)
                    after(sync, sent_by_ready, g - 1)
                    held(sync, sync_passed)
                    sync.dma_start(send_row[:, b, :],
                                   dram["dst_row"][g, :, :].to_broadcast([P, U * P])).then_inc(idx_in[b], 16)
                after(sync, gathered[b], (16 if windowed else 32) * U * i)
                held(sync, sync_passed)
                after(sync, row_f_ready, g - 1)
                held(sync, sync_passed)
                sync.dma_start(recv[:, b, :], dram["src_col"][g, :, :]).then_inc(idx_in[b], 16)
                sync.dma_start(recv_row[:, b, :, :].rearrange("p u j -> p (u j)"),
                               dram["src_row"][g, :, :].to_broadcast([P, U * P])).then_inc(idx_in[b], 16)
                if not windowed:
                    sync.dma_start(send[:, b, :], dram["dst_col"][g, :, :]).then_inc(idx_in[b], 16)

            software_pipeline(sync, tiles, G2, [(0, load)])

        def pool_program(pool, windowed):
            def gather(i, slot):
                b, u = slot // U, slot % U
                g = 2 * i + b
                if u == 0:
                    pool.wait_ge(idx_in[b], 48 * i + 48)
                    after(pool, msg_ready, g - 1)
                    held(pool, pool_passed)
                pool.indirect_dma_start(q[:, b, u, :], None, dram["q_tab"],
                                        bass.IndirectOffsetOnAxis(ap=recv[:, b, u:u + 1], axis=0)).then_inc(gathered[b], 16)
                if not windowed:
                    pool.indirect_dma_start(
                        kv[:, b, u, :], None, dram["kv_tab"],
                        bass.IndirectOffsetOnAxis(ap=send[:, b, u:u + 1], axis=0)).then_inc(gathered[b], 16)

            def scatter(i, slot):
                b, u = slot // U, slot % U
                r = slot % NREP
                k = G2 * i + slot
                pool.wait_ge(sums_ready, k + 1)
                after(pool, scattered[r], 16 * ((G2 // NREP) * i + slot // NREP))
                held(pool, pool_passed)
                pool.indirect_dma_start(dram["att_sum"][r], bass.IndirectOffsetOnAxis(ap=row[b][u][:, :], axis=0),
                                        sums[:, b, u, :], None, compute_op=ALU.add).then_inc(scattered[r], 16)

            software_pipeline(pool, tiles, G2, [(0, gather), (10, scatter)])
            for r in range(NREP):
                pool.wait_ge(scattered[r], 16 * tiles // NREP)

        def vector_program(dve, windowed):
            def senders(i, slot):
                if slot % U or not windowed:
                    return
                b = slot // U
                g = 2 * i + b
                dve.wait_ge(idx_in[b], 48 * i + 48)
                after(dve, spread, U * (g - 1))
                dve.tensor_scalar(sent_by[:, b, :, :].rearrange("p u e -> p (u e)"), send_row[:, b, :],
                                  w["node_of"][:, bass.ds(g, 1)], None, ALU.is_equal).then_inc(sent_by_ready, 1)

            def attend(i, slot):
                if slot % U:
                    return
                b = slot // U
                g = 2 * i + b
                dve.wait_ge(idx_in[b], 48 * i + 48)
                after(dve, summed, U * (g - 1))
                dve.tensor_tensor(same[:, b, :, :], recv_row[:, b, :, :],
                                  recv[:, b, :].unsqueeze(2).to_broadcast([P, U, P]), ALU.is_equal).then_inc(same_ready, 1)
                after(dve, row_ready, U * g)
                dve.tensor_scalar(off[:, :], recv[:, b, :], w["spare_f"][:, 0:1], None, ALU.subtract).then_inc(off_ready, 1)
                dve.wait_ge(same_ready, g + 1)
                dve.tensor_tensor(earlier[:, :, :], same[:, b, :, :],
                                  w["before"][:, :].unsqueeze(1).to_broadcast([P, U, P]), ALU.mult).then_inc(earlier_ready, 1)
                dve.wait_ge(earlier_ready, g + 1)
                dve.tensor_reduce(rank[:, :], earlier[:, :, :], AX.X, ALU.add).then_inc(rank_ready, 1)
                dve.wait_ge(gathered[b], (16 if windowed else 32) * U * (i + 1))
                if windowed:
                    dve.wait_ge(kv_ready, U * (g + 1))
                dve.tensor_tensor(prod[:, :, :], q[:, b, :, :], kv[:, b, :, 0:HD], ALU.mult).then_inc(prod_ready, 1)
                dve.wait_ge(rank_ready, g + 1)
                dve.tensor_scalar(first[:, :], rank[:, :], 0.0, None, ALU.is_equal).then_inc(first_ready, 1)
                dve.wait_ge(prod_ready, g + 1)
                after(dve, exp_ready, g - 1)
                dve.tensor_reduce(score[:, b, :], prod[:, :, :].rearrange("p u (h d) -> p (u h) d", h=H),
                                  AX.X, ALU.add).then_inc(score_ready, 1)
                dve.wait_ge(first_ready, g + 1)
                dve.wait_ge(off_ready, g + 1)
                dve.tensor_tensor(row_f[:, :], first[:, :], off[:, :], ALU.mult).then_inc(row_f_ready, 1)
                dve.wait_ge(row_f_ready, g + 1)
                for u in range(U):
                    scatters_done(dve, i - 1, U * b + u)
                    dve.tensor_scalar(row[b][u][:, :], row_f[:, u:u + 1], w["spare_f"][:, 0:1], None,
                                      ALU.add).then_inc(row_ready, 1)
                dve.wait_ge(exp_ready, g + 1)
                for u in range(U):
                    last = dve.tensor_tensor(
                        m[:, b, u, 0:HD].rearrange("p (h d) -> p h d", h=H),
                        kv[:, b, u, HD:2 * HD].rearrange("p (h d) -> p h d", h=H),
                        m[:, b, u, HD:AW].unsqueeze(2).to_broadcast([P, H, DK]), ALU.mult)
                last.then_inc(msg_ready, 1)

            software_pipeline(dve, tiles, G2, [(0, senders), (U, attend)])

        def scalar_program(act, windowed):
            def copy_kv(i, slot):
                if not windowed:
                    return
                b, u = slot // U, slot % U
                k = G2 * i + slot
                act.wait_ge(spread, k + 1)
                after(act, msg_ready, 2 * i + b - 1)
                act.copy(kv[:, b, u, :], ps_kv[u][:, :]).then_inc(kv_ready, 1)

            def exponentials(i, slot):
                if slot % U:
                    return
                b = slot // U
                g = 2 * i + b
                act.wait_ge(score_ready, g + 1)
                after(act, summed, U * (g - 1))
                act.activation(m[:, b, :, HD:AW], score[:, b, :].rearrange("p (u h) -> p u h", h=H),
                               ACT.Exp, scale=float(DK) ** -0.5).then_inc(exp_ready, 1)

            def copy_sums(i, slot):
                b, u = slot // U, slot % U
                k = G2 * i + slot
                act.wait_ge(summed, k + 1)
                scatters_done(act, i - 1, slot)
                act.copy(sums[:, b, u, :], ps_sum[u][:, :]).then_inc(sums_ready, 1)

            software_pipeline(act, tiles, G2, [(0, copy_kv), (U, exponentials), (G2, copy_sums)])

        def tensor_program(pe, windowed):
            def spread_kv(i, slot):
                if not windowed:
                    return
                b, u = slot // U, slot % U
                g = 2 * i + b
                k = G2 * i + slot
                if u == 0:
                    pe.wait_ge(window_in[b], 16 * (i + 1))
                    pe.wait_ge(sent_by_ready, g + 1)
                after(pe, kv_ready, k - U + 1)
                pe.matmul(ps_kv[u][:, :], sent_by[:, b, u, :], window[:, b, :], start=True, stop=True).then_inc(spread, 1)

            def add_up(i, slot):
                b, u = slot // U, slot % U
                g = 2 * i + b
                k = G2 * i + slot
                if u == 0:
                    pe.wait_ge(msg_ready, g + 1)
                    pe.wait_ge(same_ready, g + 1)
                after(pe, sums_ready, k - U + 1)
                pe.matmul(ps_sum[u][:, :], same[:, b, u, :], m[:, b, u, :], start=True, stop=True).then_inc(summed, 1)

            software_pipeline(pe, tiles, G2, [(0, spread_kv), (G2, add_up)])

        @block.sync
        def _(sync):
            by_path(sync, w["wide"], sync_program)

        @block.gpsimd
        def _(pool):
            by_path(pool, w["wide"], pool_program)

        @block.vector
        def _(dve):
            by_path(dve, w["wide"], vector_program)

        @block.scalar
        def _(act):
            by_path(act, w["wide"], scalar_program)

        @block.tensor
        def _(pe):
            by_path(pe, w["wide"], tensor_program)


def build_update(nc, w, dram, n_rows):
    tiles = n_rows // P
    with ExitStack() as ctx:
        s = Space(nc, ctx, "up_")
        part = s.sb("part", [P, 2, NREP, AW])
        tot = s.sb("tot", [P, 2, AW])
        empty = s.sb("empty", [P, 2, H])
        den = s.sb("den", [P, 2, H])
        rden = s.sb("rden", [P, 2, H])
        a = s.sb("a", [P, 2, HD])
        aT = s.sb("aT", [P, 2, 2, P])
        r1T = s.sb("r1T", [P, 2, 4, P])
        r1T_hi = s.sb("r1T_hi", [P, 2, 4, P], F32R)
        r1T_lo = s.sb("r1T_lo", [P, 2, 4, P], F32R)
        wf_hi = s.sb("wf_hi", [P, D // P, D], F32R)
        wf_lo = s.sb("wf_lo", [P, D // P, D], F32R)
        dense = s.sb("dense", [P, 2, D])
        h = s.sb("h", [P, 2, 4, MUL])
        hT = s.sb("hT", [P, 2, D])
        s_out = s.sb("s_out", [P, 2, D])
        stats = s.sb("stats", [P, 2, 6])
        mv = s.sb("mv", [P, 2, 2])
        std = s.sb("std", [P, 2, 1])
        rstd = s.sb("rstd", [P, 2, 1])
        shift = s.sb("shift", [P, 2, 1])
        ps_a = s.ps("ps_a", [P, HD])
        ps_1 = [s.ps(f"ps_1{j}", [P, 4 * P]) for j in range(2)]
        ps_2 = [s.ps(f"ps_2{j}", [P, D]) for j in range(2)]
        ps_h = s.ps("ps_h", [P, D])
        ps_s = [s.ps(f"ps_s{j}", [P, D]) for j in range(2)]
        part_in = [s.sem(f"part_in{j}") for j in range(2)]
        out_s = [s.sem(f"out_s{j}") for j in range(2)]
        names = ("tot_ready", "empty_ready", "den_ready", "rden_ready", "a_ready", "a_turned", "aT_ready", "multiplied1",
                 "r1T_ready", "hi_ready", "lo_ready", "wf_split", "multiplied2", "dense_ready", "x2_ready", "stats_ready", "mv_ready", "std_ready",
                 "rstd_ready", "shift_ready", "h_ready", "h_turned", "hT_ready", "multiplied3", "s_ready")
        (tot_ready, empty_ready, den_ready, rden_ready, a_ready, a_turned, aT_ready, multiplied1, r1T_ready,
         hi_ready, lo_ready, wf_split, multiplied2, dense_ready, x2_ready, stats_ready, mv_ready, std_ready, rstd_ready, shift_ready, h_ready,
         h_turned, hT_ready, multiplied3, s_ready) = (s.sem(n) for n in names)
        dve_passed = s.sem("dve_passed")
        block = ctx.enter_context(nc.Block())

        @block.sync
        def _(sync):
            def load(i, j):
                t = 2 * i + j
                after(sync, tot_ready, t - 1)
                for r in range(NREP):
                    sync.dma_start(part[:, j, r, :], dram["att_sum_t"][r][t, :, :]).then_inc(part_in[j], 16)

            def store(i, j):
                t = 2 * i + j
                sync.wait_ge(s_ready, t + 1)
                sync.dma_start(dram["s_tab_t"][t, :, :], s_out[:, j, :]).then_inc(out_s[j], 16)

            software_pipeline(sync, tiles, 2, [(0, load), (12, store)])
            for j in range(2):
                sync.wait_ge(out_s[j], 16 * tiles // 2)

        @block.vector
        def _(dve):
            dve.tensor_copy(wf_hi[:, :, :], w["wf"][:, :, :]).then_inc(wf_split, 1)
            dve.wait_ge(wf_split, 1)
            dve.tensor_tensor(wf_lo[:, :, :], w["wf"][:, :, :], wf_hi[:, :, :].bitcast(F32), ALU.subtract).then_inc(wf_split, 1)

            def subtract_high(i, j):
                t = 2 * i + j
                dve.wait_ge(hi_ready, t + 1)
                after(dve, multiplied2, t - 1)
                dve.tensor_tensor(r1T_lo[:, j, :, :], r1T[:, j, :, :], r1T_hi[:, j, :, :].bitcast(F32),
                                  ALU.subtract).then_inc(lo_ready, 1)

            def normalise_sums(i, j):
                t = 2 * i + j
                dve.wait_ge(part_in[j], 16 * NREP * (i + 1))
                dve.tensor_tensor(tot[:, j, :], part[:, j, 0, :], part[:, j, 1, :], ALU.add).then_inc(tot_ready, 1)
                dve.wait_ge(tot_ready, t + 1)
                dve.tensor_scalar(empty[:, j, :], tot[:, j, HD:AW], 0.0, None, ALU.is_equal).then_inc(empty_ready, 1)
                dve.wait_ge(empty_ready, t + 1)
                dve.tensor_tensor(den[:, j, :], tot[:, j, HD:AW], empty[:, j, :], ALU.add).then_inc(den_ready, 1)
                dve.wait_ge(den_ready, t + 1)
                dve.reciprocal(rden[:, j, :], den[:, j, :]).then_inc(rden_ready, 1)
                dve.wait_ge(rden_ready, t + 1)
                after(dve, a_turned, t - 1)
                dve.scalar_tensor_tensor(out=a[:, j, :].rearrange("p (h d) -> p h d", h=H),
                                         in0=tot[:, j, 0:HD].rearrange("p (h d) -> p h d", h=H), scalar=0.0,
                                         in1=rden[:, j, :].unsqueeze(2).to_broadcast([P, H, DK]),
                                         op0=ALU.max, op1=ALU.mult).then_inc(a_ready, 1)

            def add_residual(i, j):
                t = 2 * i + j
                dve.wait_ge(multiplied2, t + 1)
                dve.tensor_tensor(dense[:, j, :], ps_2[j][:, :], w["bf"][:, :], ALU.add).then_inc(dense_ready, 1)
                dve.wait_ge(dense_ready, t + 1)
                dve.scalar_tensor_tensor(out=w["xh"][:, t, :], in0=dense[:, j, :], scalar=0.0, in1=w["xh"][:, t, :],
                                         op0=ALU.max, op1=ALU.add).then_inc(x2_ready, 1)
                dve.wait_ge(x2_ready, t + 1)
                held(dve, dve_passed)
                dve.bn_stats(stats[:, j, :], w["xh"][:, t, :]).then_inc(stats_ready, 1)
                dve.wait_ge(stats_ready, t + 1)
                held(dve, dve_passed)
                after(dve, std_ready, t - 1)
                held(dve, dve_passed)
                dve.bn_aggr(mv[:, j, :], stats[:, j, :]).then_inc(mv_ready, 1)

            def scales(i, j):
                t = 2 * i + j
                dve.wait_ge(std_ready, t + 1)
                after(dve, h_ready, 2 * (t - 1))
                dve.reciprocal(rstd[:, j, :], std[:, j, :]).then_inc(rstd_ready, 1)
                dve.wait_ge(rstd_ready, t + 1)
                dve.scalar_tensor_tensor(out=shift[:, j, :], in0=mv[:, j, 0:1], scalar=-1.0, in1=rstd[:, j, :],
                                         op0=ALU.mult, op1=ALU.mult).then_inc(shift_ready, 1)

            def copy_turned(i, j):
                t = 2 * i + j
                dve.wait_ge(h_turned, t + 1)
                after(dve, multiplied3, t - 1)
                dve.tensor_copy(hT[:, j, :], ps_h[:, :]).then_inc(hT_ready, 1)

            software_pipeline(dve, tiles, 2, [(9, copy_turned), (6, scales), (0, normalise_sums), (3, subtract_high), (5, add_residual)])

        @block.scalar
        def _(act):
            def copy_aT(i, j):
                t = 2 * i + j
                act.wait_ge(a_turned, t + 1)
                after(act, multiplied1, t - 1)
                act.copy(aT[:, j, :, :].rearrange("p c n -> p (c n)"), ps_a[:, :]).then_inc(aT_ready, 1)

            def relu1(i, j):
                t = 2 * i + j
                act.wait_ge(multiplied1, t + 1)
                after(act, lo_ready, t - 1)
                for c in range(4):
                    act.activation(r1T[:, j, c, :], ps_1[j][:, c * P:(c + 1) * P], ACT.Relu,
                                   bias=w["ba"][:, c:c + 1]).then_inc(r1T_ready, 1)

            def round_r1T(i, j):
                t = 2 * i + j
                act.wait_ge(r1T_ready, 4 * (t + 1))
                after(act, multiplied2, t - 1)
                act.copy(r1T_hi[:, j, :, :], r1T[:, j, :, :]).then_inc(hi_ready, 1)

            def deviation(i, j):
                t = 2 * i + j
                act.wait_ge(mv_ready, t + 1)
                after(act, rstd_ready, t - 1)
                act.activation(std[:, j, :], mv[:, j, 1:2], ACT.Sqrt, bias=w["eps"][:, :]).then_inc(std_ready, 1)

            def normalise(i, j):
                t = 2 * i + j
                act.wait_ge(shift_ready, t + 1)
                after(act, h_turned, t - 1)
                act.activation(h[:, j, 0, :], w["xh"][:, t, 0:MUL], ACT.Relu, bias=shift[:, j, :],
                               scale=rstd[:, j, :]).then_inc(h_ready, 1)
                act.activation(h[:, j, 1:4, :], w["xh"][:, t, MUL:D].rearrange("p (u m) -> p m u", m=3), ACT.Relu,
                               bias=shift[:, j, :], scale=rstd[:, j, :]).then_inc(h_ready, 1)

            def copy_s(i, j):
                t = 2 * i + j
                act.wait_ge(multiplied3, t + 1)
                after(act, out_s[j], 16 * i)
                act.mul(s_out[:, j, :], ps_s[j][:, :], float(MUL) ** -0.5).then_inc(s_ready, 1)

            software_pipeline(act, tiles, 2, [(6, deviation), (1, copy_aT), (3, round_r1T), (2, relu1), (11, copy_s), (7, normalise)])

        @block.tensor
        def _(pe):
            pe.wait_ge(wf_split, 2)

            def turn_a(i, j):
                t = 2 * i + j
                pe.wait_ge(a_ready, t + 1)
                after(pe, aT_ready, t)
                for c in range(2):
                    last = pe.transpose(ps_a[:, c * P:(c + 1) * P], a[:, j, c * P:(c + 1) * P], w["ident"][:, :])
                last.then_inc(a_turned, 1)

            def layer1(i, j):
                t = 2 * i + j
                pe.wait_ge(aT_ready, t + 1)
                after(pe, r1T_ready, 4 * (t - 1))
                for o in range(4):
                    for c in range(2):
                        last = pe.matmul(ps_1[j][:, o * P:(o + 1) * P], w["wa"][:, c, o * P:(o + 1) * P], aT[:, j, c, :],
                                         start=(c == 0), stop=(c == 1))
                last.then_inc(multiplied1, 1)

            def layer2(i, j):
                t = 2 * i + j
                pe.wait_ge(lo_ready, t + 1)
                after(pe, dense_ready, t - 1)
                for c in range(4):
                    pe.matmul(ps_2[j][:, :], r1T_hi[:, j, c, :], wf_hi[:, c, :], start=(c == 0), stop=False)
                    pe.matmul(ps_2[j][:, :], r1T_hi[:, j, c, :], wf_lo[:, c, :], start=False, stop=False)
                    last = pe.matmul(ps_2[j][:, :], r1T_lo[:, j, c, :], wf_hi[:, c, :], start=False, stop=(c == 3))
                last.then_inc(multiplied2, 1)

            def turn_h(i, j):
                t = 2 * i + j
                pe.wait_ge(h_ready, 2 * (t + 1))
                after(pe, hT_ready, t)
                for c in range(4):
                    last = pe.transpose(ps_h[:, c * P:(c + 1) * P], h[:, j, c, :], w["ident"][:, :])
                last.then_inc(h_turned, 1)

            def up(i, j):
                t = 2 * i + j
                pe.wait_ge(hT_ready, t + 1)
                after(pe, s_ready, t - 1)
                for c in range(4):
                    last = pe.matmul(ps_s[j][:, c * P:(c + 1) * P], hT[:, j, c * P:(c + 1) * P],
                                     w["wup"][:, min(c, 1), :], start=True, stop=True)
                last.then_inc(multiplied3, 1)

            software_pipeline(pe, tiles, 2, [(1, turn_a), (2, layer1), (4, layer2), (10, up), (8, turn_h)])


def build_messages(nc, w, dram, n_edges):
    tiles = n_edges // P
    G2 = 2 * U
    with ExitStack() as ctx:
        s = Space(nc, ctx, "ms_")
        send = s.sb("send", [P, 2, U], I32)
        recv = s.sb("recv", [P, 2, U], I32)
        recv_row = s.sb("recv_row", [P, 2, U, P], I32)
        y = s.sb("y", [P, 2, U, 4])
        radial = s.sb("radial", [2 * RB, 2, 2 * P])
        h1 = s.sb("h1", [P, 2 * P])
        h2 = s.sb("h2", [P, 2 * P])
        h3 = s.sb("h3", [P, 2, U * P])
        h3_parts = s.sb("h3_parts", [P, 2, U * P], F32R)
        node = s.sb("node", [P, G2, 4, MUL])
        to = s.sb("to", [P, 2, U, P])
        to_y = s.sb("to_y", [P, 2, U, 4, P])
        place = s.sb("place", [P, 2, U])
        near = s.sb("near", [P, 2, U, SPAN])
        near_y = s.sb("near_y", [P, 2, U, 4, SPAN])
        earlier = s.sb("earlier", [P, U, P])
        rank = s.sb("rank", [P, U])
        first = s.sb("first", [P, U])
        off = s.sb("off", [P, U])
        row_f = s.sb("row_f", [P, U])
        row = [s.sb(f"row{n}", [P, 1], I32) for n in range(G2)]
        dot1 = s.sb("dot1", [P, 2, MUL])
        dot2 = s.sb("dot2", [P, MUL])
        dot = s.sb("dot", [P, 2, MUL])
        prods = s.sb("prods", [P, 2, 6, MUL])
        sums = s.sb("sums", [P, 2, MW])
        ps_h = [s.ps(f"ps_h{n}", [P, U * P]) for n in range(2)]
        ps_w = [s.ps(f"ps_w{n}", [P, 4 * MUL]) for n in range(2)]
        ps_m = [s.ps(f"ps_m{n}", [P, MW]) for n in range(2)]
        idx_in = [s.sem(f"idx_in{b}") for b in range(2)]
        mlp_in = [s.sem(f"mlp_in{b}") for b in range(2)]
        gathered = [s.sem(f"gathered{n}") for n in range(G2)]
        names = ("scattered", "place_ready", "to_ready", "earlier_ready", "rank_ready", "first_ready", "off_ready",
                 "row_f_ready", "row_ready", "to_y_ready", "dot1_ready", "dot2_ready", "dot_ready", "prods_ready",
                 "hidden", "h1_ready", "h2_ready", "h3_ready", "parts_ready", "weighed", "summed",
                 "sums_ready", "pool_passed", "sync_passed")
        (scattered, place_ready, to_ready, earlier_ready, rank_ready, first_ready, off_ready,
         row_f_ready, row_ready, to_y_ready, dot1_ready, dot2_ready, dot_ready, prods_ready,
         hidden, h1_ready, h2_ready, h3_ready, parts_ready, weighed, summed,
         sums_ready, pool_passed, sync_passed) = (s.sem(n) for n in names)
        block = ctx.enter_context(nc.Block())

        def sync_program(sync, windowed):
            def load(i, slot):
                if slot % U:
                    return
                b = slot // U
                g = 2 * i + b
                after(sync, hidden, 4 * (g - 1))
                held(sync, sync_passed)
                sync.dma_start(radial[:, b, :], dram["radial"][g, :, :]).then_inc(mlp_in[b], 16)
                if windowed:
                    after(sync, place_ready, g - 1)
                else:
                    after(sync, row_f_ready, g - 1)
                held(sync, sync_passed)
                after(sync, to_y_ready, g - 1)
                held(sync, sync_passed)
                after(sync, dot_ready, U * (g - 1))
                held(sync, sync_passed)
                for u in range(U):
                    after(sync, gathered[U * b + u], 16 * i)
                sync.dma_start(send[:, b, :], dram["src_col"][g, :, :]).then_inc(idx_in[b], 16)
                sync.dma_start(recv[:, b, :], dram["dst_col"][g, :, :]).then_inc(idx_in[b], 16)
                sync.dma_start(y[:, b, :, :].rearrange("p u k -> p (u k)"), dram["y"][g, :, :]).then_inc(idx_in[b], 16)
                if not windowed:
                    sync.dma_start(recv_row[:, b, :, :].rearrange("p u j -> p (u j)"),
                                   dram["dst_row"][g, :, :].to_broadcast([P, U * P])).then_inc(idx_in[b], 16)

            software_pipeline(sync, tiles, G2, [(0, load)])

        def indices_in(eng, i, b, windowed):
            eng.wait_ge(idx_in[b], (48 if windowed else 64) * (i + 1))

        def pool_program(pool, windowed):
            def gather(i, slot):
                b, u = slot // U, slot % U
                k = G2 * i + slot
                if u == 0:
                    indices_in(pool, i, b, windowed)
                after(pool, prods_ready, k - G2 + 1)
                held(pool, pool_passed)
                pool.indirect_dma_start(node[:, slot, :, :].rearrange("p m c -> p (m c)"), None, dram["s_tab"],
                                        bass.IndirectOffsetOnAxis(ap=send[:, b, u:u + 1], axis=0)).then_inc(gathered[slot], 16)

            def add_to_rows(i, slot):
                k = G2 * i + slot
                pool.wait_ge(sums_ready, 2 * (k + 1))
                after(pool, scattered, 16 * k)
                held(pool, pool_passed)
                pool.indirect_dma_start(dram["msg_rows"], bass.IndirectOffsetOnAxis(ap=row[slot][:, :], axis=0),
                                        sums[:, slot % 2, :], None, compute_op=ALU.add).then_inc(scattered, 16)

            def add_to_window(i, slot):
                if slot % U != U - 1:
                    return
                b = slot // U
                g = 2 * i + b
                pool.wait_ge(sums_ready, 2 * (g + 1))
                after(pool, scattered, 16 * g)
                held(pool, pool_passed)
                first_node = pool.value_load(w["base"][0:1, bass.ds(g, 1)], min_val=0, max_val=w["last_base"])
                pool.dma_start(dram["msg_cols"][:, bass.ds(first_node * 8, MW)], sums[:, b, :],
                               accum_op=ALU.add).then_inc(scattered, 16)

            if windowed:
                software_pipeline(pool, tiles, G2, [(0, gather), (G2, add_to_window)])
                pool.wait_ge(scattered, 16 * tiles // U)
            else:
                software_pipeline(pool, tiles, G2, [(0, gather), (7, add_to_rows)])
                pool.wait_ge(scattered, 16 * tiles)

        def vector_program(dve, windowed):
            def receivers(i, slot):
                if slot % U:
                    return
                b = slot // U
                g = 2 * i + b
                indices_in(dve, i, b, windowed)
                dve.tensor_tensor(place[:, b, :], recv[:, b, :], w["start"][:, bass.ds(g * U, U)],
                                  ALU.subtract).then_inc(place_ready, 1)
                dve.wait_ge(place_ready, g + 1)
                after(dve, summed, U * (g - 1))
                dve.tensor_tensor(near[:, b, :, :], w["iota_f"][:, 0:SPAN].unsqueeze(1).to_broadcast([P, U, SPAN]),
                                  place[:, b, :].unsqueeze(2).to_broadcast([P, U, SPAN]), ALU.is_equal).then_inc(to_ready, 1)
                dve.wait_ge(to_ready, g + 1)
                dve.tensor_tensor(near_y[:, b, :, :, :], near[:, b, :, :].unsqueeze(2).to_broadcast([P, U, 4, SPAN]),
                                  y[:, b, :, :].unsqueeze(3).to_broadcast([P, U, 4, SPAN]), ALU.mult).then_inc(to_y_ready, 1)

            def shared_receivers(i, slot):
                if slot % U:
                    return
                b = slot // U
                g = 2 * i + b
                indices_in(dve, i, b, windowed)
                after(dve, summed, U * (g - 1))
                dve.tensor_tensor(to[:, b, :, :], recv_row[:, b, :, :],
                                  recv[:, b, :].unsqueeze(2).to_broadcast([P, U, P]), ALU.is_equal).then_inc(to_ready, 1)
                dve.wait_ge(to_ready, g + 1)
                dve.tensor_tensor(to_y[:, b, :, :, :], to[:, b, :, :].unsqueeze(2).to_broadcast([P, U, 4, P]),
                                  y[:, b, :, :].unsqueeze(3).to_broadcast([P, U, 4, P]), ALU.mult).then_inc(to_y_ready, 1)
                dve.tensor_tensor(earlier[:, :, :], to[:, b, :, :],
                                  w["before"][:, :].unsqueeze(1).to_broadcast([P, U, P]), ALU.mult).then_inc(earlier_ready, 1)
                dve.wait_ge(earlier_ready, g + 1)
                dve.tensor_reduce(rank[:, :], earlier[:, :, :], AX.X, ALU.add).then_inc(rank_ready, 1)
                after(dve, row_ready, U * g)
                dve.tensor_scalar(off[:, :], recv[:, b, :], w["spare_f"][:, 0:1], None, ALU.subtract).then_inc(off_ready, 1)
                dve.wait_ge(rank_ready, g + 1)
                dve.tensor_scalar(first[:, :], rank[:, :], 0.0, None, ALU.is_equal).then_inc(first_ready, 1)
                dve.wait_ge(first_ready, g + 1)
                dve.wait_ge(off_ready, g + 1)
                dve.tensor_tensor(row_f[:, :], first[:, :], off[:, :], ALU.mult).then_inc(row_f_ready, 1)
                dve.wait_ge(row_f_ready, g + 1)
                for u in range(U):
                    after(dve, scattered, 16 * (U * (g - 2) + u + 1))
                    dve.tensor_scalar(row[U * b + u][:, :], row_f[:, u:u + 1], w["spare_f"][:, 0:1], None,
                                      ALU.add).then_inc(row_ready, 1)

            def split_h3(i, slot):
                if slot % U:
                    return
                b = slot // U
                g = 2 * i + b
                dve.wait_ge(h3_ready, g + 1)
                dve.tensor_tensor(h3_parts[HID:P, b, :], h3[HID:P, b, :], h3_parts[HID:P, b, :].bitcast(F32),
                                  ALU.subtract).then_inc(parts_ready, 1)

            def dots(i, slot):
                b, u, j = slot // U, slot % U, slot % 2
                k = G2 * i + slot
                dve.wait_ge(gathered[slot], 16 * (i + 1))
                dve.wait_ge(dot1_ready, k + 1)
                after(dve, dot_ready, k)
                dve.scalar_tensor_tensor(out=dot2[:, :], in0=node[:, slot, 2, :], scalar=y[:, b, u, 2:3], in1=dot1[:, j, :],
                                         op0=ALU.mult, op1=ALU.add).then_inc(dot2_ready, 1)
                dve.wait_ge(dot2_ready, k + 1)
                after(dve, prods_ready, k - 1)
                dve.scalar_tensor_tensor(out=dot[:, j, :], in0=node[:, slot, 3, :], scalar=y[:, b, u, 3:4], in1=dot2[:, :],
                                         op0=ALU.mult, op1=ALU.add).then_inc(dot_ready, 1)

            def products(i, slot):
                j = slot % 2
                k = G2 * i + slot
                dve.wait_ge(weighed, k + 1)
                after(dve, summed, k - 1)
                wts = ps_w[j][:, :].rearrange("p (w c) -> p w c", c=MUL)
                dve.tensor_tensor(prods[:, j, 0:5:4, :], wts[:, 0:2, :],
                                  node[:, slot, 0:1, :].to_broadcast([P, 2, MUL]), ALU.mult)
                dve.tensor_tensor(prods[:, j, 1:4, :], wts[:, 2:3, :].to_broadcast([P, 3, MUL]),
                                  node[:, slot, 1:4, :], ALU.mult)
                dve.wait_ge(dot_ready, k + 1)
                dve.tensor_tensor(prods[:, j, 5, :], wts[:, 3, :], dot[:, j, :], ALU.mult).then_inc(prods_ready, 1)

            receivers_stage = receivers if windowed else shared_receivers
            software_pipeline(dve, tiles, G2, [(3, receivers_stage), (4, split_h3), (5, dots), (6, products)])

        def scalar_program(act, windowed):
            def silu(i, slot):
                layer, b = (0, 1, None, 2)[slot % U], slot // U
                g = 2 * i + b
                if layer is None:
                    return
                n = 3 * b + layer
                act.wait_ge(hidden, 4 * g + (layer + 1 if layer < 2 else 4))
                if layer == 0:
                    act.activation(h1[:, :], ps_h[n % 2][:, 0:2 * P], ACT.Silu, scale=float(RB) ** -0.5).then_inc(h1_ready, 1)
                elif layer == 1:
                    act.activation(h2[:, :], ps_h[n % 2][:, 0:2 * P], ACT.Silu,
                                   scale=SILU_2MOM * float(HID) ** -0.5).then_inc(h2_ready, 1)
                else:
                    after(act, weighed, U * (g - 1))
                    act.activation(h3_parts[:, b, :], ps_h[n % 2][:, :], ACT.Silu,
                                   scale=SILU_2MOM * float(HID) ** -0.5)
                    after(act, parts_ready, g - 1)
                    act.activation(h3[HID:P, b, :], ps_h[n % 2][HID:P, :], ACT.Silu,
                                   scale=SILU_2MOM * float(HID) ** -0.5).then_inc(h3_ready, 1)

            def first_dot(i, slot):
                b, u, j = slot // U, slot % U, slot % 2
                k = G2 * i + slot
                if u == 0:
                    indices_in(act, i, b, windowed)
                act.wait_ge(gathered[slot], 16 * (i + 1))
                after(act, dot2_ready, k - 1)
                act.activation(dot1[:, j, :], node[:, slot, 1, :], ACT.Copy, scale=y[:, b, u, 1:2]).then_inc(dot1_ready, 1)

            def copy_group(i, slot):
                if slot % U != U - 1:
                    return
                b = slot // U
                g = 2 * i + b
                act.wait_ge(summed, U * (g + 1))
                after(act, scattered, 16 * (g - 1))
                for half in range(2):
                    act.copy(sums[:, b, :].rearrange("p (n k) -> p k n", k=8)[:, half * 4:(half + 1) * 4, :],
                             ps_m[b][:, half * D:(half + 1) * D].rearrange("p (k n) -> p k n", k=4)).then_inc(sums_ready, 1)

            def copy_tile(i, slot):
                k = G2 * i + slot
                act.wait_ge(summed, k + 1)
                after(act, scattered, 16 * (k - 1))
                for half in range(2):
                    act.copy(sums[:, slot % 2, half * D:(half + 1) * D],
                             ps_m[slot % 2][:, half * D:(half + 1) * D]).then_inc(sums_ready, 1)

            if windowed:
                software_pipeline(act, tiles, G2, [(0, silu), (4, first_dot), (7, copy_group)])
            else:
                software_pipeline(act, tiles, G2, [(0, silu), (4, first_dot), (7, copy_tile)])

        def tensor_program(pe, windowed):
            def mlp(i, slot):
                layer, b = (0, 1, 2, 2)[slot % U], slot // U
                half = slot % U - 2
                g = 2 * i + b
                n = 3 * b + layer
                if layer == 0:
                    pe.wait_ge(mlp_in[b], 16 * (i + 1))
                    after(pe, h2_ready, g)
                    pe.matmul(ps_h[n % 2][:, 0:2 * P], w["mlp1"][:, :], radial[:, b, :],
                              start=True, stop=True).then_inc(hidden, 1)
                elif layer == 1:
                    pe.wait_ge(h1_ready, g + 1)
                    after(pe, h3_ready, g)
                    pe.matmul(ps_h[n % 2][:, 0:2 * P], w["mlp2"][:, :], h1[:, :], start=True, stop=True).then_inc(hidden, 1)
                else:
                    pe.wait_ge(h2_ready, g + 1)
                    pe.matmul(ps_h[n % 2][:, half * 2 * P:(half + 1) * 2 * P], w["mlp3"][:, half, :], h2[:, :],
                              start=True, stop=True).then_inc(hidden, 1)

            def weigh(i, slot):
                b, u = slot // U, slot % U
                g = 2 * i + b
                k = G2 * i + slot
                if u == 0:
                    pe.wait_ge(parts_ready, g + 1)
                after(pe, prods_ready, k - 1)
                parts = h3_parts[:, b, u * P:(u + 1) * P]
                pe.matmul(ps_w[slot % 2][:, :], parts, w["mlp4_hi"][:, :], start=True, stop=False)
                pe.matmul(ps_w[slot % 2][:, :], parts, w["mlp4_lo"][:, :],
                          start=False, stop=True).then_inc(weighed, 1)

            def add_up(i, slot):
                b, u, j = slot // U, slot % U, slot % 2
                g = 2 * i + b
                k = G2 * i + slot
                if u == 0:
                    pe.wait_ge(to_y_ready, g + 1)
                pe.wait_ge(prods_ready, k + 1)
                after(pe, sums_ready, 2 * (k - 1))
                pe.matmul(ps_m[j][:, 0:4 * MUL], to_y[:, b, u, 0, :],
                          prods[:, j, 0:4, :].rearrange("p m c -> p (m c)"), start=True, stop=True)
                for m in range(3):
                    pe.matmul(ps_m[j][:, (4 + m) * MUL:(5 + m) * MUL], to_y[:, b, u, 1 + m, :], prods[:, j, 4, :],
                              start=True, stop=True)
                pe.matmul(ps_m[j][:, 7 * MUL:8 * MUL], to[:, b, u, :], prods[:, j, 5, :],
                          start=True, stop=True).then_inc(summed, 1)

            def add_up_window(i, slot):
                b, u, j = slot // U, slot % U, slot % 2
                g = 2 * i + b
                k = G2 * i + slot
                if u == 0:
                    after(pe, sums_ready, 2 * (g - 1))
                    for half in range(2):
                        pe.matmul(ps_m[b][:, half * D:(half + 1) * D], w["zero"][:, 0:P], w["zero"][:, :],
                                  start=True, stop=False, skip_group_check=True)
                    pe.wait_ge(to_y_ready, g + 1)
                offset = pe.value_load(w["offset"][0:1, bass.ds(k, 1)], min_val=0, max_val=P - SPAN)
                pe.wait_ge(prods_ready, k + 1)
                blocks = ps_m[b][:, :].rearrange("p (k n) -> p k n", k=8)

                def add(first, count, product, places):
                    return pe.matmul(blocks[:, first:first + count, bass.ds(offset, SPAN)], prods[:, j, product, :],
                                     places, start=False, stop=(u == U - 1), skip_group_check=True)

                for block_of_row in range(4):
                    add(block_of_row, 1, block_of_row, near_y[:, b, u, 0:1, :])
                add(4, 3, 4, near_y[:, b, u, 1:4, :])
                add(7, 1, 5, near[:, b, u:u + 1, :]).then_inc(summed, 1)

            add_up_stage = add_up_window if windowed else add_up
            software_pipeline(pe, tiles, G2, [(0, mlp), (6, weigh), (7, add_up_stage)])

        @block.sync
        def _(sync):
            by_path(sync, w["wide"], sync_program)

        @block.gpsimd
        def _(pool):
            by_path(pool, w["wide"], pool_program)

        @block.vector
        def _(dve):
            by_path(dve, w["wide"], vector_program)

        @block.scalar
        def _(act):
            by_path(act, w["wide"], scalar_program)

        @block.tensor
        def _(pe):
            by_path(pe, w["wide"], tensor_program)


def build_output(nc, w, dram, n_rows):
    tiles = n_rows // P
    TERMS = [((0, 0), (7, 1)), ((4, 2), (1, 3)), ((5, 2), (2, 3)), ((6, 2), (3, 3))]
    with ExitStack() as ctx:
        s = Space(nc, ctx, "ou_")
        tot = s.sb("tot", [P, 4, MW])
        totT = s.sb("totT", [P, 2, MW])
        out = s.sb("out", [P, 2, D])
        ps_t = [s.ps(f"ps_t{n}", [P, D]) for n in range(4)]
        ps_o = [s.ps(f"ps_o{n}", [P, D]) for n in range(4)]
        tot_in = [s.sem(f"tot_in{n}") for n in range(4)]
        stored = [s.sem(f"stored{j}") for j in range(2)]
        turned, totT_ready, multiplied, out_ready = (s.sem(n) for n in (
            "turned", "totT_ready", "multiplied", "out_ready"))
        block = ctx.enter_context(nc.Block())

        def sync_program(sync, windowed):
            def load(i, n):
                t = 4 * i + n
                if windowed:
                    after(sync, multiplied, t - 3)
                    sync.dma_start(tot[:, n, :], dram["msg_cols"][:, bass.ds(t * MW, MW)]).then_inc(tot_in[n], 16)
                else:
                    after(sync, turned, 2 * (t - 3))
                    sync.dma_start(tot[:, n, :], dram["msg_rows_t"][t, :, :]).then_inc(tot_in[n], 16)

            def store(i, n):
                t = 4 * i + n
                sync.wait_ge(out_ready, 2 * (t + 1))
                sync.dma_start(dram["out_t"][t, :, :], out[:, n % 2, :]).then_inc(stored[n % 2], 16)

            software_pipeline(sync, tiles, 4, [(0, load), (4, store)])
            for j in range(2):
                sync.wait_ge(stored[j], 16 * tiles // 2)

        def vector_program(dve, windowed):
            def add_residual(i, n):
                t = 4 * i + n
                dve.wait_ge(multiplied, t + 1)
                after(dve, stored[n % 2], 16 * (2 * i + n // 2))
                dve.tensor_tensor(out[:, n % 2, 0:MUL], ps_o[n][:, 0:MUL], w["xh"][:, t, 0:MUL],
                                  ALU.add).then_inc(out_ready, 1)
                dve.tensor_tensor(out[:, n % 2, MUL:D].rearrange("p (v m) -> p m v", m=3),
                                  ps_o[n][:, MUL:D].rearrange("p (m v) -> p m v", m=3),
                                  w["xh"][:, t, MUL:D].rearrange("p (v m) -> p m v", m=3), ALU.add).then_inc(out_ready, 1)

            software_pipeline(dve, tiles, 4, [(0, add_residual)])

        def scalar_program(act, windowed):
            def copy_turned(i, n):
                t = 4 * i + n
                for half in range(2):
                    act.wait_ge(turned, 2 * t + half + 1)
                    after(act, multiplied, t - 1)
                    act.copy(totT[:, n % 2, half * D:(half + 1) * D], ps_t[2 * (n % 2) + half][:, :]).then_inc(totT_ready, 1)

            if not windowed:
                software_pipeline(act, tiles, 4, [(0, copy_turned)])

        def tensor_program(pe, windowed):
            def turn(i, n):
                t = 4 * i + n
                pe.wait_ge(tot_in[n], 16 * (i + 1))
                after(pe, totT_ready, 2 * (t - 1))
                for half in range(2):
                    for c in range(4):
                        last = pe.transpose(ps_t[2 * (n % 2) + half][:, c * P:(c + 1) * P],
                                            tot[:, n, half * D + c * P:half * D + (c + 1) * P], w["ident"][:, :])
                    last.then_inc(turned, 1)

            def multiply(i, n):
                t = 4 * i + n
                if windowed:
                    pe.wait_ge(tot_in[n], 16 * (i + 1))
                    by_block = tot[:, n, :].rearrange("p (r k) -> p k r", k=8)
                else:
                    pe.wait_ge(totT_ready, 2 * (t + 1))
                    by_block = totT[:, n % 2, :].rearrange("p (k r) -> p k r", k=8)
                after(pe, out_ready, 2 * (t - 3))
                for o, terms in enumerate(TERMS):
                    for a, (block_of_row, weight) in enumerate(terms):
                        last = pe.matmul(ps_o[n][:, o * MUL:(o + 1) * MUL], by_block[:, block_of_row, :],
                                         w["wout"][:, weight, :], start=(a == 0), stop=(a == 1))
                last.then_inc(multiplied, 1)

            software_pipeline(pe, tiles, 4, [(0, multiply)] if windowed else [(0, turn), (1, multiply)])

        @block.sync
        def _(sync):
            by_path(sync, w["wide"], sync_program)

        @block.vector
        def _(dve):
            by_path(dve, w["wide"], vector_program)

        @block.scalar
        def _(act):
            by_path(act, w["wide"], scalar_program)

        @block.tensor
        def _(pe):
            by_path(pe, w["wide"], tensor_program)


def build(nc, dram, n_rows, n_edges):
    groups = n_edges // (U * P)

    def scratch(name, shape, dt=F32):
        return nc.dram_tensor(name, shape, dt, kind="Internal").ap()

    dram["q_tab"] = scratch("q_tab", (n_rows, HD))
    dram["kv_tab"] = scratch("kv_tab", (n_rows, 2 * HD))
    dram["s_tab"] = scratch("s_tab", (n_rows, D))
    dram["att_sum"] = [scratch(f"att_sum{r}", (n_rows, AW)) for r in range(NREP)]
    msg_sum = scratch("msg_sum", (n_rows * MW,))
    dram["msg_rows"] = msg_sum.rearrange("(n k) -> n k", k=MW)
    dram["msg_cols"] = msg_sum.rearrange("(c k) -> c k", c=P)
    dram["base"] = scratch("base", (1, groups), I32)
    dram["offset"] = scratch("offset", (1, groups * U), I32)
    dram["start"] = scratch("start", (1, groups * U))
    dram["span"] = scratch("span", (1, groups * U), I32)
    by_tile = "(t p) n -> t p n"
    for name in ("q_tab", "kv_tab", "s_tab", "msg_rows", "out"):
        dram[name + "_t"] = dram[name].rearrange(by_tile, p=P)
    dram["att_sum_t"] = [table.rearrange(by_tile, p=P) for table in dram["att_sum"]]

    with ExitStack() as ctx:
        s = Space(nc, ctx, "w_")
        w = {
            "xh": s.sb("xh", [P, n_rows // P, D]),
            "mlp1": s.sb("mlp1", [2 * RB, P]),
            "mlp2": s.sb("mlp2", [P, P]),
            "mlp3": s.sb("mlp3", [P, 2, P]),
            "mlp4_hi": s.sb("mlp4_hi", [P, 4 * MUL], F32R),
            "mlp4_lo": s.sb("mlp4_lo", [P, 4 * MUL], F32R),
            "wout": s.sb("wout", [P, 4, MUL]),
            "ident": s.sb("ident", [P, P]),
            "before": s.sb("before", [P, P]),
            "iota_f": s.sb("iota_f", [P, P]),
            "spare_f": s.sb("spare_f", [P, 1]),
            "base": s.sb("base", [P, groups], I32),
            "start": s.sb("start", [P, groups * U]),
            "offset": s.sb("offset", [1, groups * U], I32),
            "zero": s.sb("zero", [P, 4 * MUL], BF16),
            "node_of": s.sb("node_of", [P, groups]),
            "wide": s.sb("wide", [1, 1], I32),
            "last_base": n_rows - P,
        }
        with ExitStack() as first_layer:
            s = Space(nc, first_layer, "w_")
            w |= {
                "wa": s.sb("wa", [P, HD // P, D]),
                "ba": s.sb("ba", [P, D // P]),
                "wf": s.sb("wf", [P, D // P, D]),
                "bf": s.sb("bf", [P, D]),
                "wup": s.sb("wup", [P, 2, MUL]),
                "eps": s.sb("eps", [P, 1]),
            }
            with ExitStack() as projection:
                s = Space(nc, projection, "w_")
                w |= {
                    "wqkv_hi": s.sb("wqkv_hi", [P, D // P, 3 * HD], F32R),
                    "wqkv_lo": s.sb("wqkv_lo", [P, D // P, 3 * HD], F32R),
                    "bqkv": s.sb("bqkv", [P, 3 * HD]),
                    "zeros": s.sb("zeros", [P, MW]),
                }
                build_setup(nc, w, dram, n_rows, groups)
                build_project(nc, w, dram, n_rows)
            build_attention(nc, w, dram, n_edges)
            build_update(nc, w, dram, n_rows)
        build_messages(nc, w, dram, n_edges)
        build_output(nc, w, dram, n_rows)


WEIGHTS = ["L0_gnn_Wk", "L0_gnn_bk", "L0_gnn_Wq", "L0_gnn_bq", "L0_gnn_Wv", "L0_gnn_bv", "L0_gnn_Wa", "L0_gnn_ba",
           "L0_gnn_Wf", "L0_gnn_bf", "L1_gnn_W_up0", "L1_gnn_W_up1", "L1_gnn_W_mlp1", "L1_gnn_W_mlp2",
           "L1_gnn_W_mlp3", "L1_gnn_W_mlp4", "L1_gnn_W_out0", "L1_gnn_W_out1"]


def layout(inputs):
    import numpy as np

    x = np.asarray(inputs["x"])
    src, dst = np.asarray(inputs["src"]), np.asarray(inputs["dst"])
    n, e = x.shape[0], src.shape[0]
    n_rows, n_edges = node_rows(n), edge_rows(e)
    groups = n_edges // (U * P)
    arrays = {name: np.ascontiguousarray(inputs[name]) for name in WEIGHTS}
    xp = np.zeros((n_rows, D), x.dtype)
    xp[:n] = x
    arrays["x"] = xp.reshape(n_rows // P, P, D)
    for name, a in (("src", src), ("dst", dst)):
        full = np.full(n_edges, n, a.dtype)
        full[:e] = a
        arrays[name + "_row"] = full.reshape(groups, 1, U * P)
        arrays[name + "_col"] = np.ascontiguousarray(full.reshape(groups, U, P).transpose(0, 2, 1))
    y = np.asarray(inputs["edge_attr_4"])
    full = np.zeros((n_edges, 4), y.dtype)
    full[:e] = y
    arrays["y"] = np.ascontiguousarray(full.reshape(groups, U, P, 4).transpose(0, 2, 1, 3)).reshape(groups, P, U * 4)
    radial = np.asarray(inputs["edge_attr_8"])
    full = np.zeros((n_edges, RB), radial.dtype)
    full[:e] = radial
    arrays["radial"] = np.ascontiguousarray(
        full.reshape(groups, 2, 2 * P, RB).transpose(0, 1, 3, 2)).reshape(groups, 2 * RB, 2 * P)
    return arrays, n_rows, n_edges


def kernel(**inputs):
    import numpy as np
    import concourse.bacc as bacc
    from concourse.bass_utils import run_bass_kernel_spmd

    arrays, n_rows, n_edges = layout(inputs)
    nc = bacc.Bacc("TRN2", target_bir_lowering=False, num_devices=1)
    dram, by_name = {}, {}
    for name, a in arrays.items():
        by_name[f"in_{name}"] = a
        dram[name] = nc.dram_tensor(f"in_{name}", a.shape, mybir.dt.from_np(a.dtype), kind="ExternalInput").ap()
    dram["out"] = nc.dram_tensor("out", (n_rows, D), F32, kind="ExternalOutput").ap()
    build(nc, dram, n_rows, n_edges)
    result = run_bass_kernel_spmd(nc, [by_name], core_ids=[0])
    return result.results[0]["out"][:np.asarray(inputs["x"]).shape[0]]
```
